# Optimizing a Trainium2 kernel written in Bass

```python
import numpy as np
import jax
import jax.numpy as jnp

def _softmax(x, axis=-1):
    return jax.nn.softmax(x, axis=axis)

def _gelu(x):
    return jax.nn.gelu(x, approximate=True)

def _silu(x):
    return jax.nn.silu(x)

def _sigmoid(x):
    return jax.nn.sigmoid(x)

def _layernorm(x, axis=-1, eps=1e-05):
    m = jnp.mean(x, axis=axis, keepdims=True)
    v = jnp.var(x, axis=axis, keepdims=True)
    return (x - m) / jnp.sqrt(v + eps)

def _scatter_add(tgt, idx, src, axis=0):
    return tgt.at[idx].add(src)

def _segment_sum(src, seg, n):
    return jax.ops.segment_sum(src, seg, n)
kernel_name = 'mk_xattn_ffn_d1_seqx_r4_236a9b'

def setup_inputs(seed: int=0):
    np.random.seed(seed)
    _w = jnp.asarray

    def _rec_inputs():
        import jax
        import jax.numpy as jnp
        _rk = jax.random.key(seed)
        x = -0.0002928 + 1 * jax.random.normal(jax.random.fold_in(_rk, 1), (2, 1024, 256), jnp.float32)
        _lenS = 1024 - jax.random.randint(jax.random.fold_in(_rk, 7), (2,), 0, max(1, 1024 // 4) + 1, jnp.int32)
        _lenS2 = 154 - jax.random.randint(jax.random.fold_in(_rk, 8), (2,), 0, max(1, 154 // 4) + 1, jnp.int32)
        _ctx_1024P = jax.random.normal(jax.random.fold_in(_rk, 11), (2, 16, 256), jnp.float32)
        _ctx_1024c = jax.random.dirichlet(jax.random.fold_in(_rk, 511), 0.3 * jnp.ones((16,), jnp.float32), (2, 154))
        _ctx_1024t = jnp.einsum('bsk,bkd->bsd', _ctx_1024c, _ctx_1024P)
        _ctx_1024t = _ctx_1024t * jax.lax.rsqrt(jnp.mean(jnp.square(_ctx_1024t)) + 1e-12) * 0.953939
        ctx_1024 = 0.000227908 + 0.99994 * (_ctx_1024t + 0.3 * jax.random.normal(jax.random.fold_in(_rk, 611), (2, 154, 256), jnp.float32))
        return (x, ctx_1024)
    x, ctx_1024 = _rec_inputs()

    def _L0_xattn_setup():
        import jax, jax.numpy as jnp
        import numpy as np
        HEADS = 16
        key = jax.random.key(seed)
        ks = jax.random.split(key, 6)
        b, n, m, dim = (2, 512, 128, 256)
        s = dim ** (-0.5)
        return {'x': jax.random.normal(ks[0], (b, n, dim), jnp.float32), 'mem': jax.random.normal(ks[1], (b, m, dim), jnp.float32), 'Wq': jax.random.normal(ks[2], (dim, dim), jnp.float32) * s, 'Wkv': jax.random.normal(ks[3], (dim, 2 * dim), jnp.float32) * s, 'Wout': jax.random.normal(ks[4], (dim, dim), jnp.float32) * s, 'bout': jnp.zeros((dim,), jnp.float32)}
    _L0_xattn_all = _L0_xattn_setup()
    _L0_xattn_in = {k: v for k, v in _L0_xattn_all.items() if k in ('Wq', 'Wkv', 'Wout', 'bout')}
    del _L0_xattn_all

    def _L0_ffn_setup():
        import jax, jax.numpy as jnp
        import numpy as np
        key = jax.random.key(seed)
        k0, k1, k2, k3 = jax.random.split(key, 4)
        B, S, D, F, E = (8, 512, 256, 512, 8)
        x = jax.random.normal(k0, (B, S, D), dtype=jnp.float32)
        Wg = jax.random.normal(k1, (D, E), dtype=jnp.float32) * 0.02
        W1 = jax.random.normal(k2, (E, D, F), dtype=jnp.float32) * 0.02
        W2 = jax.random.normal(k3, (E, F, D), dtype=jnp.float32) * 0.02
        return {'x': x, 'Wg': Wg, 'W1': W1, 'W2': W2}
    _L0_ffn_all = _L0_ffn_setup()
    _L0_ffn_in = {k: v for k, v in _L0_ffn_all.items() if k in ('Wg', 'W1', 'W2')}
    del _L0_ffn_all
    return {'x': x, 'ctx_1024': ctx_1024, 'L0_xattn_Wq': _L0_xattn_in['Wq'], 'L0_xattn_Wkv': _L0_xattn_in['Wkv'], 'L0_xattn_Wout': _L0_xattn_in['Wout'], 'L0_xattn_bout': _L0_xattn_in['bout'], 'L0_ffn_Wg': _L0_ffn_in['Wg'], 'L0_ffn_W1': _L0_ffn_in['W1'], 'L0_ffn_W2': _L0_ffn_in['W2']}

def reference(x, ctx_1024, L0_xattn_Wq, L0_xattn_Wkv, L0_xattn_Wout, L0_xattn_bout, L0_ffn_Wg, L0_ffn_W1, L0_ffn_W2):
    import jax
    import jax.numpy as jnp

    def _L0_xattn_ref(x, mem, Wq, Wkv, Wout, bout):
        import jax, jax.numpy as jnp
        import numpy as np
        HEADS = 16
        b, n, dim = x.shape
        h = HEADS
        d = dim // h
        scale = d ** (-0.5)
        mem_len = mem.shape[1]
        q = x @ Wq
        xc = jnp.concatenate((mem, x), axis=1)
        kv = xc @ Wkv
        k, v = jnp.split(kv, 2, axis=-1)

        def to_heads(t):
            bb, nn, _ = t.shape
            return t.reshape(bb, nn, h, d).transpose(0, 2, 1, 3)
        q, k, v = (to_heads(q), to_heads(k), to_heads(v))
        dots = jnp.einsum('bhid,bhjd->bhij', q, k) * scale
        j = dots.shape[-1]
        i_idx = jnp.arange(n)[:, None]
        j_idx = jnp.arange(j)[None, :]
        mask = j_idx > i_idx + mem_len
        dots = jnp.where(mask[None, None], -jnp.inf, dots)
        attn = jax.nn.softmax(dots, axis=-1)
        out = jnp.einsum('bhij,bhjd->bhid', attn, v)
        out = out.transpose(0, 2, 1, 3).reshape(b, n, dim)
        return out @ Wout + bout

    def _L0_ffn_ref(x, Wg, W1, W2):
        import jax, jax.numpy as jnp
        import numpy as np
        B, S, D = x.shape
        E = Wg.shape[1]
        T = B * S
        cap = max(1, T // E)
        xt = x.reshape(T, D)
        logits = xt @ Wg
        probs = jax.nn.softmax(logits, axis=-1)
        pT = probs.T
        _, top_idx = jax.lax.top_k(pT, cap)
        sel = jnp.zeros((E, T), dtype=bool).at[jnp.arange(E)[:, None], top_idx].set(True)
        masked = jnp.where(sel, pT, -jnp.inf)
        assigned = sel.any(axis=0)
        tok2exp = jnp.where(assigned, jnp.argmax(masked, axis=0), jnp.argmax(pT, axis=0))
        weights = jnp.take_along_axis(probs, tok2exp[:, None], axis=1)[:, 0]
        out = jnp.zeros_like(xt)
        for e in range(E):
            gate = jnp.where(tok2exp == e, weights, 0.0)
            h = jax.nn.gelu(xt @ W1[e], approximate=False) @ W2[e]
            out = out + gate[:, None] * h
        return out.reshape(B, S, D)
    x = x + _L0_xattn_ref(_layernorm(x, axis=-1), ctx_1024, L0_xattn_Wq, L0_xattn_Wkv, L0_xattn_Wout, L0_xattn_bout)
    x = x + _L0_ffn_ref(_layernorm(x, axis=-1), L0_ffn_Wg, L0_ffn_W1, L0_ffn_W2)
    return x

_drawn_inputs = setup_inputs


def setup_inputs(seed=0):
    import zlib

    import numpy as np

    out = dict(_drawn_inputs(seed))
    spreads = {'L0_xattn_bout': (0.0, 0.1)}
    factors = {'L0_ffn_Wg': 4.095, 'L0_ffn_W1': 3.907, 'L0_ffn_W2': 3.83}
    for name, (base, spread) in spreads.items():
        noise = np.random.default_rng([zlib.crc32(name.encode()), seed]).standard_normal(out[name].shape)
        drawn = base * np.exp(spread * noise) if base else spread * noise
        out[name] = jnp.asarray(drawn.astype(out[name].dtype))
    for name, factor in factors.items():
        out[name] = (out[name] * factor).astype(out[name].dtype)
    return out
```

```python
from contextlib import ExitStack

import concourse.bass as bass
from concourse import mybir

F32 = mybir.dt.float32
BF16 = mybir.dt.bfloat16
I32 = mybir.dt.int32
U32 = mybir.dt.uint32
ALU = mybir.AluOpType
ACT = mybir.ActivationFunctionType
AX = mybir.AxisListType

P = 128
NB = 2
S = 1024
M = 154
D = 256
KT = D // P
H = 16
HD = D // H
NG = 4
GH = H // NG
J = M + S
JT = -(-J // P)
JP = JT * P
QT = S // P
T = NB * S
TT = T // P
E = 8
F = 512
FT = F // P
CAP = T // E
NS = (T + E * (P - 1)) // P + 1
SCALE = float(HD) ** -0.5
EPS = 1e-5
NPROD = 6
QPART = [0, 0, 1, 1, 0, 2]
KPART = [0, 1, 0, 1, 2, 0]
KROWS = NPROD * HD
SROWS = KROWS + 2
VC = 32
SAFE = 40.0
NEG = -1.0e30

def first_query(t):
    return max(0, t * P - M)

STEPS = [[(t, first_query(t), first_query(t))] for t in range(7)]
STEPS.append([])
_col = 0
for _t in range(7, JT):
    STEPS[-1].append((_t, first_query(_t), _col))
    _col += S - first_query(_t)
NSTEP = len(STEPS)
def max_pieces(qt):
    width, out = M + P * (qt + 1), []
    while width > 0:
        n = min(512, width)
        out.append((width - n, n))
        width -= n
    return out[::-1]

NPIECE = sum(len(max_pieces(qt)) for qt in range(QT))


def split_at_bank(c0, c1):
    out = []
    while c0 < c1:
        c = min(c1, (c0 // 512 + 1) * 512)
        out.append((c0, c))
        c0 = c
    return out


def xattn_ffn(nc, x, ctx, Wq, Wkv, Wout, bout, Wg, W1, W2, out, xs, ys, force_shift=False):
    es = ExitStack()
    with es:
        def sb(name, shape, dt=F32):
            return es.enter_context(nc.sbuf_tensor(name, shape, dt))

        def sem(name):
            return es.enter_context(nc.semaphore(name))

        xres = sb("xres", [P, TT, D])
        QN, KN, VN = NB * KT * 3 * S // 2, NB * KT * 3 * J // 2, NB * JT * D
        big = sb("big", [P, QN + KN + VN])
        q_parts = big[:, 0:QN].bitcast(BF16).rearrange("p (b m c n) -> p b m c n", b=NB, m=KT, c=3)
        k_parts = big[:, QN:QN + KN].bitcast(BF16).rearrange("p (b m c n) -> p b m c n", b=NB, m=KT, c=3)
        v_all = big[:, QN + KN:QN + KN + VN].rearrange("p (b t n) -> p b t n", b=NB, t=JT)
        w1_sb = big[:, 0:E * KT * F]
        w2_sb = big[:, E * KT * F:E * KT * F + E * FT * D]
        mid = sb("mid", [P, NB * NG * S])
        xcT = mid[:, 0:NB * KT * JP].rearrange("p (b k n) -> p b k n", b=NB, k=KT)
        oT = mid[:, :].rearrange("p (b g n) -> p b g n", b=NB, g=NG)
        c0 = NB * KT * JP
        bias = mid[:, c0:c0 + D]
        zrow = mid[:, c0 + D:c0 + 2 * D]
        icol = mid[:, c0 + 2 * D:c0 + 2 * D + P].bitcast(I32)
        ic2 = mid[:, c0 + 2 * D + P:c0 + 2 * D + 2 * P].bitcast(I32)
        q_st = [sb(f"q_st{i}", [SROWS, GH, S], BF16) for i in range(2)]
        k_st = [sb(f"k_st{i}", [SROWS, GH, JP], BF16) for i in range(2)]
        v_st = [sb(f"v_st{i}", [P, JT, GH, VC]) for i in range(2)]
        pbuf = sb("pbuf", [P, 2, GH, S])
        flat = pbuf[:, :, :, :].rearrange("p a h n -> p (a h n)")
        xn = flat[:, 0:TT * D].rearrange("p (t n) -> p t n", t=TT)
        ctx_sb = flat[:, TT * D:TT * D + NB * 2 * D].rearrange("p (b t n) -> p b t n", b=NB, t=2)
        WK0 = TT * D
        c0 = WK0 + NB * 2 * D
        wq_sb = flat[:, c0:c0 + KT * D].rearrange("p (k n) -> p k n", k=KT)
        c0 += KT * D
        wkv_sb = flat[:, c0:c0 + KT * 2 * D].rearrange("p (k n) -> p k n", k=KT)
        c0 += KT * 2 * D
        rem = flat[:, c0:c0 + 1024].rearrange("p (a n) -> p a n", a=2)
        c0 += 1024
        sq = flat[:, c0:c0 + 512].bitcast(BF16).rearrange("p (a n) -> p a n", a=2)
        wout_sb = sb("wout_sb", [P, KT, D])
        wg_sb = sb("wg_sb", [P, KT, E])
        ident = sb("ident", [P, P])
        ident_b = sb("ident_b", [P, P], BF16)
        tri = sb("tri", [P, P], BF16)
        heads = sb("heads", [P, P], BF16)
        same_e = sb("same_e", [P, P], BF16)
        prev_e = sb("prev_e", [P, P], BF16)
        before = sb("before", [P, P], BF16)
        ones_b = sb("ones_b", [P, P], BF16)
        seen = sb("seen", [P, P])
        irow = sb("irow", [P, 1], I32)
        ir2 = sb("ir2", [P, 1], I32)
        fcol = sb("fcol", [P, P])
        frow = sb("frow", [P, 4])
        stats = sb("stats", [P, TT, 6])
        mv = sb("mv", [P, TT, 2])
        ve = sb("ve", [P, TT])
        rstd = sb("rstd", [P, TT])
        nt1 = sb("nt1", [P, TT])
        n2 = sb("n2", [P, 20])
        bnd = sb("bnd", [P, 8])
        flag = sb("flag", [P, 1], I32)
        mx = sb("mx", [P, GH, QT, 3])
        mrow = sb("mrow", [P, GH, QT])
        shift = sb("shift", [P, QT, GH, 2], BF16)
        shiftT = sb("shiftT", [2 * GH, S], BF16)

        ps = es.enter_context(nc.psum_tensor("ps", [P, 4096], F32))

        def bank(i):
            return ps[:, 512 * i:512 * i + 512]

        st_ps = [ps[:, 0:1024], ps[:, 1024:2048]]
        o_ps = [ps[:, 2048:3072], ps[:, 3072:4096]]

        x_in = [sem(f"x_in{i}") for i in range(4)]
        ctx_in = sem("ctx_in")
        w_in = sem("w_in")
        bias_in = sem("bias_in")
        const_made = sem("const_made")
        dve_step = sem("dve_step")
        ve_done = sem("ve_done")
        sqrt_done = sem("sqrt_done")
        xn_done = sem("xn_done")
        pad_done = sem("pad_done")
        tr_ready = sem("tr_ready")
        tr_done = sem("tr_done")
        proj_ready = sem("proj_ready")
        hi_done = sem("hi_done")
        lo_done = sem("lo_done")
        mid_done = sem("mid_done")
        low_done = sem("low_done")
        vcopy_done = sem("vcopy_done")
        sq_done = sem("sq_done")
        norm_ready = sem("norm_ready")
        norm_done = sem("norm_done")
        bound_done = sem("bound_done")
        all_max = sem("all_max")
        flag_done = sem("flag_done")
        ones_rows = sem("ones_rows")
        zfill = sem("zfill")
        qk_in = [sem(f"qk_in{i}") for i in range(2)]
        v_in = sem("v_in")
        st_ready = sem("st_ready")
        exp_done = sem("exp_done")
        mask_done = sem("mask_done")
        pv_done = sem("pv_done")
        o_free = sem("o_free")
        mx_ready = sem("mx_ready")
        mx_done = sem("mx_done")
        sh_done = sem("sh_done")
        shT_ready = sem("shT_ready")
        shT_done = sem("shT_done")
        sh_in = sem("sh_in")
        w1_in = sem("w1_in")
        w2_in = sem("w2_in")
        ot_ready = sem("ot_ready")
        on_done = sem("on_done")
        ont_ready = sem("ont_ready")
        ont_done = sem("ont_done")
        wo_ready = sem("wo_ready")
        x1_done = sem("x1_done")
        ve2_done = sem("ve2_done")
        sqrt2_done = sem("sqrt2_done")
        xn2_done = sem("xn2_done")
        xt2_ready = sem("xt2_ready")
        xt2_done = sem("xt2_done")
        lg_ready = sem("lg_ready")
        lsub_done = sem("lsub_done")
        lexp_done = sem("lexp_done")
        probs_done = sem("probs_done")
        pt_ready = sem("pt_ready")
        cnt_done = sem("cnt_done")
        tot_ready = sem("tot_ready")
        sel_done = sem("sel_done")
        selT_ready = sem("selT_ready")
        hot_done = sem("hot_done")
        rank_ready = sem("rank_ready")
        pos_done = sem("pos_done")
        scat = sem("scat")
        xs_in = [sem(f"xs_in{i}") for i in range(2)]
        fx_ready = sem("fx_ready")
        fx_done = sem("fx_done")
        fh_ready = sem("fh_ready")
        fg_done = sem("fg_done")
        ft_ready = sem("ft_ready")
        ft_done = sem("ft_done")
        fy_ready = sem("fy_ready")
        fy_done = sem("fy_done")
        ys_out = [sem(f"ys_out{i}") for i in range(2)]
        gath = sem("gath")
        res_done = sem("res_done")
        out_done = sem("out_done")

        def proj_jobs(b):
            jobs = [("q", m, n0, 512) for m in range(KT) for n0 in range(0, S, 512)]
            jobs += [("k", m, n0, min(512, J - n0)) for m in range(KT) for n0 in range(0, J, 512)]
            jobs += [("v", t, 0, 0) for t in range(0, JT, 2)]
            return [(b,) + j for j in jobs]

        JOBS = proj_jobs(0) + proj_jobs(1)
        QKJ = [n for n, j in enumerate(JOBS) if j[1] != "v"]
        VJ = [n for n, j in enumerate(JOBS) if j[1] == "v"]

        base = [WK0]

        def work(*dims, dt=F32):
            n = 1
            for d in dims:
                n *= d
            a = flat[:, base[0]:base[0] + n]
            base[0] += n
            if dt != F32:
                a = a.bitcast(dt)
            return a
        on_sb = flat[:, WK0:WK0 + 2 * D].rearrange("p (a n) -> p a n", a=2)
        onT_sb = flat[:, WK0 + 2 * D:WK0 + 4 * D].rearrange("p (a n) -> p a n", a=2)
        xs_sb = [work(D) for _ in range(2)]
        xT_sb = [work(D) for _ in range(2)]
        h_sb = [work(F) for _ in range(2)]
        hT_sb = [work(F) for _ in range(2)]
        y_sb = [work(D) for _ in range(2)]
        assert base[0] <= 2 * GH * S
        rt = v_st[0][:, :, :, :].rearrange("p t h c -> p (t h c)")
        rbase = [0]

        def rwork(n, dt=F32):
            a = rt[:, rbase[0]:rbase[0] + n]
            rbase[0] += n
            return a if dt == F32 else a.bitcast(dt)
        TE = TT * E
        r_probs = rwork(TE)
        r_max = rwork(TT)
        r_PT = rwork(P)
        r_junk = rwork(P)
        r_eq = rwork(P)
        r_sel = rwork(P)
        r_one = rwork(P)
        r_tmp = rwork(TE)
        r_hot = rwork(TE)
        rt1 = v_st[1][:, :, :, :].rearrange("p t h c -> p (t h c)")
        rt, rbase = rt1, [0]
        r_te = rwork(TE)
        r_inc = rwork(TE)
        r_reset = rwork(TE)
        r_iota = rwork(24)
        r_i128 = rwork(16)
        r_e8 = rwork(8)
        r_nt = rwork(8)
        r_end = rwork(8)
        r_pos = rwork(TT)
        r_any = rwork(TT)
        r_gate = rwork(TT)
        r_tx = rwork(NS * E)
        r_hotb = rwork(TE // 2, BF16)
        r_posu = sb("r_posu", [P, TT], U32)
        r_texp = sb("r_texp", [P, NS], I32)
        cand = sb("cand", [P, 1], I32)
        mstep = sb("mstep", [P, 1], I32)
        cnt_b = sb("cnt_b", [P, 4], BF16)
        lim = sb("lim", [P, 2])
        rec = sb("rec", [P, 2, H])

        blk = es.enter_context(nc.Block())

        @blk.sync
        def _(sp):
            xr = x.rearrange("b (t p) d -> p (b t) d", p=P)
            for i in range(4):
                n = TT // 4
                sp.dma_start(xres[:, i * n:(i + 1) * n, :], xr[:, i * n:(i + 1) * n, :]).then_inc(x_in[i], 16)
            sp.dma_start(wq_sb[:, :, :], Wq.rearrange("(k p) n -> p k n", p=P)).then_inc(w_in, 16)
            sp.dma_start(wkv_sb[:, :, :], Wkv.rearrange("(k p) n -> p k n", p=P)).then_inc(w_in, 16)
            sp.dma_start(wout_sb[:, :, :], Wout.rearrange("(k p) n -> p k n", p=P)).then_inc(w_in, 16)
            sp.dma_start(wg_sb[:, :, :], Wg.rearrange("(k p) n -> p k n", p=P)).then_inc(w_in, 16)
            sp.dma_start(bias[:, :], bout.partition_broadcast(P)).then_inc(bias_in, 16)
            sp.wait_ge(const_made, 1)
            for i in range(NS):
                sp.dma_start(xs[i * P:(i + 1) * P, :], zrow[:, :]).then_inc(zfill, 16)

            def stage(pa, b, m):
                for c in range(NPROD):
                    for r in range(GH):
                        lo = 64 * pa + HD * r
                        sp.dma_start(q_st[pa][HD * c:HD * c + HD, r, :],
                                     q_parts[lo:lo + HD, bass.ds(b, 1), bass.ds(m, 1), QPART[c], :]).then_inc(qk_in[pa], 16)
                        sp.dma_start(k_st[pa][HD * c:HD * c + HD, r, 0:J],
                                     k_parts[lo:lo + HD, bass.ds(b, 1), bass.ds(m, 1), KPART[c], :]).then_inc(qk_in[pa], 16)

            sp.wait_ge(hi_done, len(QKJ))
            sp.wait_ge(mid_done, len(QKJ))
            sp.wait_ge(low_done, len(QKJ))
            sp.wait_ge(ones_rows, 2)
            for pa in range(2):
                stage(pa, 0, 0)

            def shift_rows(sp, pa, seen):
                sp.wait_ge(shT_done, seen)
                for r in range(GH):
                    sp.dma_start(q_st[pa][KROWS:SROWS, r, :], shiftT[2 * r:2 * r + 2, :]).then_inc(sh_in, 16)

            sp.wait_ge(flag_done, 1)
            fl = sp.value_load(flag[0:1, 0:1], min_val=0, max_val=1)
            with sp.Fori(0, NG - 1) as it:
                for pa in range(2):
                    with sp.If(fl > 0):
                        shift_rows(sp, pa, it * 2 + pa + 1)
                for pa in range(2):
                    sp.wait_ge(pv_done, it * (2 * NSTEP) + NSTEP * (pa + 1) + 2)
                    stage(pa, (it + 1) // 2, (it + 1) % 2)
            for pa in range(2):
                with sp.If(fl > 0):
                    shift_rows(sp, pa, 2 * (NG - 1) + pa + 1)
            sp.wait_ge(qk_in[0], 16 * 48 * NG)
            sp.wait_ge(qk_in[1], 16 * 48 * NG)
            sp.wait_ge(v_in, 2 * NG)
            for e in range(E):
                sp.dma_start(w1_sb[:, e * KT * F:(e + 1) * KT * F].rearrange("p (k n) -> p k n", k=KT),
                             W1[e].rearrange("(k p) n -> p k n", p=P)).then_inc(w1_in, 16)
                sp.dma_start(w2_sb[:, e * FT * D:(e + 1) * FT * D].rearrange("p (k n) -> p k n", k=FT),
                             W2[e].rearrange("(k p) n -> p k n", p=P)).then_inc(w2_in, 16)
            sp.wait_ge(scat, 16 * TT)
            for k in range(2):
                sp.dma_start(xs_sb[k], xs[k * P:(k + 1) * P, :]).then_inc(xs_in[k], 16)
            with sp.Fori(0, NS // 2 - 1) as it:
                for pa in range(2):
                    sp.wait_ge(fx_ready, it * 2 + pa + 1)
                    sp.dma_start(xs_sb[pa], xs[bass.ds(it * (2 * P) + (2 + pa) * P, P), :]).then_inc(xs_in[pa], 16)
                    sp.wait_ge(fy_done, it * 2 + pa + 1 + 2)
                    sp.dma_start(ys[bass.ds(it * (2 * P) + pa * P, P), :], y_sb[pa]).then_inc(ys_out[pa], 16)
            for pa in range(2):
                sp.wait_ge(fy_done, NS - 2 + pa + 1 + 2)
                k = NS - 2 + pa
                sp.dma_start(ys[k * P:(k + 1) * P, :], y_sb[pa]).then_inc(ys_out[pa], 16)
            outr = out.rearrange("b (t p) d -> p (b t) d", p=P)
            for t in range(TT):
                sp.wait_ge(res_done, t + 1)
                sp.dma_start(outr[:, t, :], xres[:, t, :]).then_inc(out_done, 16)
            sp.wait_ge(out_done, 16 * TT)

        @blk.gpsimd
        def _(pool):
            nc.gpsimd.memset(zrow[:, :], 0.0).then_inc(const_made, 1)
            pool.dma_start(ctx_sb[:, :, 0, :], ctx[:, 0:P, :].rearrange("b p d -> p b d")).then_inc(ctx_in, 16)
            pool.dma_start(ctx_sb[0:M - P, :, 1, :], ctx[:, P:M, :].rearrange("b p d -> p b d")).then_inc(ctx_in, 16)
            nc.gpsimd.memset(ident[:, :], 0.0).then_inc(const_made, 1)
            pool.wait_ge(const_made, 2)
            nc.gpsimd.affine_select(out=ident[:, :], in_=ident[:, :], compare_op=ALU.not_equal, fill=1.0,
                                    base=0, pattern=[[-1, P]], channel_multiplier=1).then_inc(const_made, 1)
            nc.gpsimd.memset(tri[:, :], 0.0).then_inc(const_made, 1)
            pool.wait_ge(const_made, 4)
            nc.gpsimd.affine_select(out=tri[:, :], in_=tri[:, :], compare_op=ALU.is_ge, fill=NEG,
                                    base=0, pattern=[[-1, P]], channel_multiplier=1).then_inc(const_made, 1)
            nc.gpsimd.iota(icol[:, :], pattern=[[1, P]], base=0, channel_multiplier=0).then_inc(const_made, 1)
            nc.gpsimd.iota(irow[:, :], pattern=[[0, 1]], base=0, channel_multiplier=1).then_inc(const_made, 1)
            for i in range(2):
                nc.gpsimd.memset(k_st[i][:, :, :], 0.0).then_inc(const_made, 1)
                nc.gpsimd.memset(q_st[i][:, :, :], 0.0).then_inc(const_made, 1)
                nc.gpsimd.memset(v_st[i][:, :, :, :], 0.0).then_inc(const_made, 1)
            pool.wait_ge(const_made, 13)
            for i in range(2):
                nc.gpsimd.memset(v_st[i][:, 0:JT - 1, :, HD:HD + 1], 1.0).then_inc(const_made, 1)
                pool.wait_ge(const_made, 14 + 2 * i)
                nc.gpsimd.memset(v_st[i][0:J - (JT - 1) * P, JT - 1, :, HD:HD + 1], 1.0).then_inc(const_made, 1)
                pool.wait_ge(const_made, 15 + 2 * i)
                nc.gpsimd.memset(k_st[i][KROWS:SROWS, :, 0:J], 1.0).then_inc(ones_rows, 1)
                pool.wait_ge(ones_rows, i + 1)
            n = 0
            for jn, (b, kind, m, n0, w) in enumerate(JOBS):
                if kind == "v":
                    continue
                pool.wait_ge(mid_done, n + 1)
                dst = (q_parts if kind == "q" else k_parts)
                nc.gpsimd.tensor_tensor(dst[:, b, m, 2, n0:n0 + w], rem[:, n % 2, 0:w],
                                        dst[:, b, m, 1, n0:n0 + w], ALU.subtract).then_inc(low_done, 1)
                n += 1
            pool.wait_ge(bound_done, 1)
            nc.gpsimd.partition_all_reduce(bnd[:, 1:2], bnd[:, 0:1], P, bass.bass_isa.ReduceOp.max).then_inc(all_max, 1)

            def load_v(pa, b, m):
                g = 2 * m + pa
                pool.wait_ge(const_made, 17)
                nc.gpsimd.tensor_copy(v_st[pa][:, :, :, 0:HD],
                                      v_all[:, bass.ds(b, 1), :, bass.ds(g * (GH * HD), GH * HD)]
                                      .rearrange("p b t (h c) -> p (b t) h c", h=GH)).then_inc(v_in, 1)

            pool.wait_ge(vcopy_done, len(VJ))
            for pa in range(2):
                load_v(pa, 0, 0)
            with pool.Fori(0, NG - 1) as it:
                for pa in range(2):
                    pool.wait_ge(pv_done, it * (2 * NSTEP) + NSTEP * (pa + 1) + 2)
                    load_v(pa, (it + 1) // 2, (it + 1) % 2)
            pool.wait_ge(pos_done, 1)
            pool.wait_ge(zfill, 16 * NS)
            for t in range(TT):
                pool.indirect_dma_start(xs[:, :], bass.IndirectOffsetOnAxis(r_posu[:, t:t + 1], 0),
                                        xn[:, t, :], None).then_inc(scat, 16)
            for pa in range(2):
                pool.wait_ge(ys_out[pa], 16 * (NS // 2))
            for t in range(TT):
                pool.indirect_dma_start(xn[:, t, :], None, ys[:, :],
                                        bass.IndirectOffsetOnAxis(r_posu[:, t:t + 1], 0)).then_inc(gath, 16)
            pool.wait_ge(gath, 16 * TT)

        @blk.scalar
        def _(act):
            act.wait_ge(ve_done, 1)
            nc.scalar.activation(rstd[:, :], ve[:, :], ACT.Sqrt).then_inc(sqrt_done, 1)
            n = 0
            for b in range(NB):
                for q4 in range(2):
                    for k in range(KT):
                        act.wait_ge(tr_ready, n + 1)
                        nc.scalar.copy(xcT[:, b, k, M + 512 * q4:M + 512 * q4 + 512], bank(n % 8)).then_inc(tr_done, 1)
                        n += 1
                act.wait_ge(tr_ready, n + 1)
                nc.scalar.copy(xcT[:, b, :, 0:M], bank(n % 8)[:, 0:KT * M].rearrange("p (k n) -> p k n", k=KT)).then_inc(tr_done, 1)
                n += 1
            nq = nv = 0
            for jn, (b, kind, m, n0, w) in enumerate(JOBS):
                act.wait_ge(proj_ready, jn + 1)
                if kind == "v":
                    nc.scalar.copy(v_all[:, b, m:m + 2, :], bank(jn % 7).rearrange("p (t n) -> p t n", t=2)).then_inc(vcopy_done, 1)
                    nv += 1
                else:
                    dst = (q_parts if kind == "q" else k_parts)
                    nc.scalar.copy(dst[:, b, m, 0, n0:n0 + w], bank(jn % 7)[:, 0:w]).then_inc(hi_done, 1)
                    if nq >= 2:
                        act.wait_ge(norm_ready, nq - 1)
                    act.activation(sq[:, nq % 2, 0:w], bank(jn % 7)[:, 0:w], ACT.Square).then_inc(sq_done, 1)
                    nq += 1

            def exps(g0):
                for s in range(NSTEP):
                    c0 = STEPS[s][0][2]
                    c1 = S if s < NSTEP - 1 else sum(S - q0 for _, q0, _ in STEPS[s])
                    for r in range(GH):
                        act.wait_ge(st_ready, (g0 * NSTEP + s) * GH + r + 1)
                        if r == 0:
                            act.wait_ge(pv_done, g0 * NSTEP + s + 1)
                        nc.scalar.activation(pbuf[:, s % 2, r, c0:c1], st_ps[r % 2][:, c0:c1], ACT.Exp,
                                             scale=SCALE).then_inc(exp_done, 1)

            with act.Fori(0, NG) as it:
                for pa in range(2):
                    exps(it * 2 + pa)
            for t in range(TT):
                act.wait_ge(ont_ready, t + 1)
                if t >= 2:
                    act.wait_ge(wo_ready, t - 1)
                nc.scalar.copy(onT_sb[:, t % 2, :], bank(2 + t % 2)[:, 0:D]).then_inc(ont_done, 1)
            act.wait_ge(ve2_done, 1)
            nc.scalar.activation(rstd[:, :], ve[:, :], ACT.Sqrt).then_inc(sqrt2_done, 1)
            for t in range(TT):
                act.wait_ge(xt2_ready, t + 1)
                if t >= 2:
                    act.wait_ge(lg_ready, t - 1)
                nc.scalar.copy(onT_sb[:, t % 2, :], bank(2 + t % 2)[:, 0:D]).then_inc(xt2_done, 1)
            act.wait_ge(lsub_done, 1)
            nc.scalar.activation(r_probs, r_probs, ACT.Exp).then_inc(lexp_done, 1)

            def ffn_x(pa, k):
                act.wait_ge(fx_ready, k + 1)
                act.wait_ge(fh_ready, k - 1 + 2)
                nc.scalar.copy(xT_sb[pa], bank(pa)[:, 0:D]).then_inc(fx_done, 1)

            def ffn_h(pa, k):
                act.wait_ge(fh_ready, k + 1 + 2)
                act.wait_ge(ft_ready, k - 1 + 2)
                nc.scalar.activation(h_sb[pa], bank(2 + pa), ACT.Gelu).then_inc(fg_done, 1)

            ffn_x(0, 0)
            ffn_h(0, 0)
            with act.Fori(0, NS // 2 - 1) as it:
                ffn_x(1, it * 2 + 1)
                ffn_h(1, it * 2 + 1)
                ffn_x(0, it * 2 + 2)
                ffn_h(0, it * 2 + 2)
            ffn_x(1, NS - 1)
            ffn_h(1, NS - 1)

        @blk.tensor
        def _(pe):
            pe.sem_inc(exp_done, 2)
            pe.sem_inc(pv_done, 2)
            pe.sem_inc(fh_ready, 2)
            pe.sem_inc(ft_ready, 2)
            pe.wait_ge(const_made, 17)
            pe.wait_ge(xn_done, TT)
            pe.wait_ge(ctx_in, 32)
            n = 0
            for b in range(NB):
                for q4 in range(2):
                    for k in range(KT):
                        if n >= 8:
                            pe.wait_ge(tr_done, n - 7)
                        for i in range(4):
                            last = nc.tensor.transpose(bank(n % 8)[:, i * P:(i + 1) * P],
                                                       xn[:, b * QT + 4 * q4 + i, k * P:(k + 1) * P], ident[:, :])
                        last.then_inc(tr_ready, 1)
                        n += 1
                if n >= 8:
                    pe.wait_ge(tr_done, n - 7)
                for k in range(KT):
                    nc.tensor.transpose(bank(n % 8)[:, k * M:k * M + P], ctx_sb[:, b, 0, k * P:(k + 1) * P], ident[:, :])
                    last = nc.tensor.transpose(bank(n % 8)[:, k * M + P:k * M + M],
                                               ctx_sb[0:M - P, b, 1, k * P:(k + 1) * P], ident[0:M - P, 0:M - P])
                last.then_inc(tr_ready, 1)
                n += 1
            pe.wait_ge(w_in, 64)
            pe.wait_ge(tr_done, n)
            pe.wait_ge(pad_done, 1)

            def norms(n):
                w = JOBS[QKJ[n]][4]
                pe.wait_ge(sq_done, n + 1)
                if n >= 1:
                    pe.wait_ge(norm_done, n)
                nc.tensor.matmul(bank(7)[:, 0:w], heads[:, :], sq[:, n % 2, 0:w], start=True, stop=True).then_inc(norm_ready, 1)

            normed = 0
            pe.wait_ge(pad_done, 3)
            for jn, (b, kind, m, n0, w) in enumerate(JOBS):
                bk, prev = jn % 7, jn - 7
                if prev >= 0:
                    if JOBS[prev][1] == "v":
                        pe.wait_ge(vcopy_done, VJ.index(prev) + 1)
                    else:
                        pe.wait_ge(lo_done, QKJ.index(prev) + 1)
                if kind == "v":
                    for i in range(2):
                        for k in range(KT):
                            last = nc.tensor.matmul(bank(bk)[:, i * D:(i + 1) * D], xcT[:, b, k, (m + i) * P:(m + i + 1) * P],
                                                    wkv_sb[:, k, D:2 * D], start=(k == 0), stop=(k == KT - 1))
                else:
                    for k in range(KT):
                        w_ap = (wq_sb if kind == "q" else wkv_sb)[:, k, m * P:(m + 1) * P]
                        c0 = n0 + (M if kind == "q" else 0)
                        last = nc.tensor.matmul(bank(bk)[:, 0:w], w_ap, xcT[:, b, k, c0:c0 + w],
                                                start=(k == 0), stop=(k == KT - 1))
                last.then_inc(proj_ready, 1)
                while normed < len(QKJ) and QKJ[normed] <= jn - 2:
                    norms(normed)
                    normed += 1
            while normed < len(QKJ):
                norms(normed)
                normed += 1
            pe.wait_ge(vcopy_done, len(VJ))
            pe.wait_ge(lo_done, len(QKJ))
            pe.wait_ge(norm_done, len(QKJ))

            def scores(pa, s, r, g0):
                pe.wait_ge(exp_done, (g0 * NSTEP + s) * GH + r + 1)
                for (t, q0, c0) in STEPS[s]:
                    for (a, z) in split_at_bank(c0, c0 + S - q0):
                        last = nc.tensor.matmul(st_ps[r % 2][:, a:z], k_st[pa][:, r, t * P:(t + 1) * P],
                                                q_st[pa][:, r, q0 + a - c0:q0 + z - c0], start=True, stop=True)
                last.then_inc(st_ready, 1)

            def values(pa, s, g0):
                if s == 0:
                    pe.wait_ge(o_free, g0 + 1)
                    pe.wait_ge(v_in, g0 + 1)
                    pe.wait_ge(exp_done, (g0 * NSTEP + s) * GH + GH + 2)
                else:
                    pe.wait_ge(mask_done, g0 * ((NSTEP - 1) * GH) + s * GH)
                for (t, q0, c0) in STEPS[s]:
                    for (a, z) in split_at_bank(q0, S):
                        for r in range(GH):
                            last = nc.tensor.matmul(o_ps[pa][32 * r:32 * r + 32, a:z], v_st[pa][:, t, r, :],
                                                    pbuf[:, s % 2, r, c0 + a - q0:c0 + z - q0],
                                                    start=(t == 0), stop=(t == JT - 1), skip_group_check=True)
                last.then_inc(pv_done, 1)

            def maxima(pa, g0):
                i = 0
                for r in range(GH):
                    for qt in range(QT):
                        for (c0, w) in max_pieces(qt):
                            pe.wait_ge(mx_done, g0 * (GH * NPIECE) + i + 1)
                            b0 = o_ps[pa][:, 512 * (i % 2):512 * (i % 2) + w]
                            dg = c0 + w == M + P * (qt + 1)
                            last = nc.tensor.matmul(b0, q_st[pa][0:KROWS, r, qt * P:(qt + 1) * P],
                                                    k_st[pa][0:KROWS, r, c0:c0 + w], start=True, stop=True, skip_group_check=True)
                            if dg:
                                last = nc.tensor.matmul(b0[:, w - P:w], ident_b[:, :], tri[:, :], start=False, stop=True,
                                                        skip_group_check=True)
                            last.then_inc(mx_ready, 1)
                            i += 1
                pe.wait_ge(sh_done, g0 + 1)
                bt = o_ps[pa][0:2 * GH, 0:512].bitcast(BF16)
                for qt in range(QT):
                    last = nc.tensor.transpose(bt[:, qt * P:(qt + 1) * P],
                                               shift[:, qt, :, :].rearrange("p h c -> p (h c)"), ident_b[:, :])
                last.then_inc(shT_ready, 1)
                pe.wait_ge(sh_in, g0 * (16 * GH) + 16 * GH)

            pe.wait_ge(flag_done, 1)
            fl = pe.value_load(flag[0:1, 0:1], min_val=0, max_val=1)
            with pe.Fori(0, NG) as it:
                for pa in range(2):
                    g0 = it * 2 + pa
                    pe.wait_ge(qk_in[pa], it * (16 * 48) + 16 * 48)
                    with pe.If(fl > 0):
                        pe.wait_ge(o_free, g0 + 1)
                        maxima(pa, g0)
                    for s in range(NSTEP + 1):
                        if s < NSTEP:
                            scores(pa, s, 0, g0)
                            scores(pa, s, 1, g0)
                        if s > 0:
                            values(pa, s - 1, g0)
                        if s < NSTEP:
                            scores(pa, s, 2, g0)
                            scores(pa, s, 3, g0)
            pe.wait_ge(o_free, 2 * NG + 2)

            def back(t):
                pe.wait_ge(on_done, t + 1)
                if t >= 2:
                    pe.wait_ge(ont_done, t - 1)
                for k in range(KT):
                    last = nc.tensor.transpose(bank(2 + t % 2)[:, k * P:(k + 1) * P], on_sb[:, t % 2, k * P:(k + 1) * P], ident[:, :])
                last.then_inc(ont_ready, 1)

            def wout(t):
                pe.wait_ge(ont_done, t + 1)
                if t >= 2:
                    pe.wait_ge(x1_done, t - 1)
                for k in range(KT):
                    last = nc.tensor.matmul(bank(4 + t % 2)[:, 0:D], onT_sb[:, t % 2, k * P:(k + 1) * P], wout_sb[:, k, :],
                                            start=(k == 0), stop=(k == KT - 1))
                last.then_inc(wo_ready, 1)

            for t in range(TT + 2):
                if t < TT:
                    if t >= 2:
                        pe.wait_ge(on_done, t - 1)
                    for g in range(NG):
                        last = nc.tensor.transpose(bank(t % 2)[:, g * P:(g + 1) * P],
                                                   oT[:, t // QT, g, (t % QT) * P:(t % QT + 1) * P], ident[:, :])
                    last.then_inc(ot_ready, 1)
                if 1 <= t <= TT:
                    back(t - 1)
                if t >= 2:
                    wout(t - 2)
            def logits(t):
                pe.wait_ge(xt2_done, t + 1)
                for k in range(KT):
                    last = nc.tensor.matmul(bank(6)[:, t * E:(t + 1) * E], onT_sb[:, t % 2, k * P:(k + 1) * P], wg_sb[:, k, :],
                                            start=(k == 0), stop=(k == KT - 1))
                last.then_inc(lg_ready, 1)

            for t in range(TT + 1):
                if t < TT:
                    pe.wait_ge(xn2_done, t + 1)
                    if t >= 2:
                        pe.wait_ge(xt2_done, t - 1)
                    for k in range(KT):
                        last = nc.tensor.transpose(bank(2 + t % 2)[:, k * P:(k + 1) * P], xn[:, t, k * P:(k + 1) * P], ident[:, :])
                    last.then_inc(xt2_ready, 1)
                if t >= 1:
                    logits(t - 1)
            pe.wait_ge(probs_done, 1)
            nc.tensor.transpose(bank(0)[:, 0:P], r_probs, ident[:, :]).then_inc(pt_ready, 1)
            for i in range(30):
                pe.wait_ge(cnt_done, i + 1)
                nc.tensor.matmul(bank(1)[:, 0:1], same_e[:, :], cnt_b[:, 0:1], start=True, stop=True).then_inc(tot_ready, 1)
            pe.wait_ge(cnt_done, 31)
            nc.tensor.matmul(bank(1)[:, 0:1], same_e[:, :], cnt_b[:, 1:2], start=True, stop=True)
            nc.tensor.matmul(bank(2)[:, 0:1], prev_e[:, :], cnt_b[:, 2:3], start=True, stop=True).then_inc(tot_ready, 1)
            pe.wait_ge(sel_done, 1)
            nc.tensor.transpose(bank(0)[:, 0:P], r_sel, ident[:, :]).then_inc(selT_ready, 1)
            pe.wait_ge(hot_done, 1)
            nc.tensor.matmul(bank(1)[:, 0:TE], before[:, :], r_hotb, start=True, stop=True)
            nc.tensor.matmul(bank(2)[:, 0:TE], ones_b[:, :], r_hotb, start=True, stop=True).then_inc(rank_ready, 1)

            def ffn_xt(pa, nth, k):
                pe.wait_ge(xs_in[pa], nth)
                for kk in range(KT):
                    last = nc.tensor.transpose(bank(pa)[:, kk * P:(kk + 1) * P], xs_sb[pa][:, kk * P:(kk + 1) * P], ident[:, :])
                last.then_inc(fx_ready, 1)

            def ffn_w1(pa, k):
                e = pe.value_load(r_texp[0:1, bass.ds(k, 1)], min_val=0, max_val=E - 1)
                pe.wait_ge(fx_done, k + 1)
                for kk in range(KT):
                    last = nc.tensor.matmul(bank(2 + pa), xT_sb[pa][:, kk * P:(kk + 1) * P],
                                            w1_sb[:, bass.ds(e * (KT * F) + kk * F, F)], start=(kk == 0), stop=(kk == KT - 1))
                last.then_inc(fh_ready, 1)

            def ffn_ht(pa, k):
                pe.wait_ge(fg_done, k + 1)
                pe.wait_ge(ft_done, k - 1 + 2)
                for kk in range(FT):
                    last = nc.tensor.transpose(bank(4 + pa)[:, kk * P:(kk + 1) * P], h_sb[pa][:, kk * P:(kk + 1) * P], ident[:, :])
                last.then_inc(ft_ready, 1)

            def ffn_w2(pa, k):
                e = pe.value_load(r_texp[0:1, bass.ds(k, 1)], min_val=0, max_val=E - 1)
                pe.wait_ge(ft_done, k + 1 + 2)
                pe.wait_ge(fy_done, k - 1 + 2)
                for kk in range(FT):
                    last = nc.tensor.matmul(bank(6 + pa)[:, 0:D], hT_sb[pa][:, kk * P:(kk + 1) * P],
                                            w2_sb[:, bass.ds(e * (FT * D) + kk * D, D)], start=(kk == 0), stop=(kk == FT - 1))
                last.then_inc(fy_ready, 1)

            pe.wait_ge(w1_in, 16 * E)
            pe.wait_ge(w2_in, 16 * E)
            pe.wait_ge(pos_done, 1)
            ffn_xt(0, 16, 0)
            ffn_w1(0, 0)

            def tile_pair(it, last):
                k = it * 2
                ffn_xt(1, it * 16 + 16, k + 1)
                ffn_ht(0, k)
                ffn_w1(1, k + 1)
                ffn_w2(0, k)
                if not last:
                    ffn_xt(0, it * 16 + 32, k + 2)
                ffn_ht(1, k + 1)
                if not last:
                    ffn_w1(0, k + 2)
                ffn_w2(1, k + 1)

            with pe.Fori(0, NS // 2 - 1) as it:
                tile_pair(it, False)
            tile_pair(NS // 2 - 1, True)

        @blk.vector
        def _(v):
            steps = [0]

            def seq(ins):
                steps[0] += 1
                ins.then_inc(dve_step, 1)
                v.wait_ge(dve_step, steps[0])

            v.sem_inc(o_free, 2)
            v.sem_inc(ft_done, 2)
            v.sem_inc(fy_done, 2)
            v.sem_inc(mx_done, 2)
            for t in range(TT):
                if t % 4 == 0:
                    v.wait_ge(x_in[t // 4], 16)
                ins = nc.vector.bn_stats(stats[:, t, :], xres[:, t, :])
            seq(ins)
            for t in range(TT):
                ins = nc.vector.bn_aggr(mv[:, t, :], stats[:, t, :])
            seq(ins)

            def normalise(tag_done, sq_sem, src, done):
                nc.vector.tensor_scalar_add(ve[:, :], mv[:, :, 1], EPS).then_inc(tag_done, 1)
                v.wait_ge(sq_sem, 1)
                seq(nc.vector.reciprocal(rstd[:, :], rstd[:, :]))
                seq(nc.vector.tensor_tensor(nt1[:, :], rstd[:, :], rstd[:, :], ALU.mult))
                seq(nc.vector.tensor_tensor(nt1[:, :], nt1[:, :], ve[:, :], ALU.mult))
                seq(nc.vector.tensor_scalar(nt1[:, :], nt1[:, :], -0.5, 1.5, ALU.mult, ALU.add))
                seq(nc.vector.tensor_tensor(rstd[:, :], rstd[:, :], nt1[:, :], ALU.mult))
                for t in range(TT):
                    nc.vector.tensor_scalar(xn[:, t, :], src[:, t, :], mv[:, t, 0:1], rstd[:, t:t + 1],
                                            ALU.subtract, ALU.mult).then_inc(done, 1)

            normalise(ve_done, sqrt_done, xres, xn_done)
            nc.vector.memset(xcT[:, :, :, J:JP], 0.0).then_inc(pad_done, 1)
            v.wait_ge(bias_in, 16)
            v.wait_ge(xn_done, TT)
            seq(nc.vector.tensor_tensor(xres[:, :, :], xres[:, :, :],
                                        bias[:, None, :].broadcast_to([P, TT, D]), ALU.add))
            v.wait_ge(const_made, 7)
            seq(nc.vector.tensor_copy(ident_b[:, :], ident[:, :]))

            def rc(col_op, col_v, row_op, row_v):
                if col_op is None:
                    seq(nc.vector.tensor_copy(fcol[:, :], icol[:, :]))
                    seq(nc.vector.tensor_copy(frow[:, 0:1], irow[:, :]))
                else:
                    seq(nc.vector.tensor_scalar(ic2[:, :], icol[:, :], col_v, None, col_op))
                    seq(nc.vector.tensor_scalar(ir2[:, :], irow[:, :], row_v, None, row_op))
                    seq(nc.vector.tensor_copy(fcol[:, :], ic2[:, :]))
                    seq(nc.vector.tensor_copy(frow[:, 0:1], ir2[:, :]))

            rc(ALU.logical_shift_right, 4, ALU.logical_shift_right, 4)
            seq(nc.vector.tensor_scalar(heads[:, :], fcol[:, :], frow[:, 0:1], None, ALU.is_equal))
            rc(ALU.bitwise_and, E - 1, ALU.bitwise_and, E - 1)
            seq(nc.vector.tensor_scalar(same_e[:, :], fcol[:, :], frow[:, 0:1], None, ALU.is_equal))
            rc(ALU.logical_shift_right, 3, ALU.logical_shift_right, 3)
            seq(nc.vector.tensor_scalar(prev_e[:, :], fcol[:, :], frow[:, 0:1], None, ALU.is_gt))
            seq(nc.vector.tensor_tensor(prev_e[:, :], prev_e[:, :], same_e[:, :], ALU.mult))
            rc(None, 0, None, 0)
            seq(nc.vector.tensor_scalar(before[:, :], fcol[:, :], frow[:, 0:1], None, ALU.is_gt))
            seq(nc.vector.tensor_scalar(seen[:, :], fcol[:, :], frow[:, 0:1], None, ALU.is_ge))
            nc.vector.memset(ones_b[:, :], 1.0).then_inc(pad_done, 1)
            nc.vector.memset(mx[:, :, :, :], -3.0e38).then_inc(pad_done, 1)

            def norm_max(i):
                v.wait_ge(norm_ready, i + 1)
                nc.vector.reduce_max(n2[:, i:i + 1], bank(7)[:, 0:JOBS[QKJ[i]][4]], AX.X).then_inc(norm_done, 1)

            nq = 0
            for jn, (b, kind, m, n0, w) in enumerate(JOBS):
                if kind == "v":
                    continue
                dst = (q_parts if kind == "q" else k_parts)
                v.wait_ge(hi_done, nq + 1)
                v.wait_ge(sq_done, nq + 1)
                if nq >= 2:
                    v.wait_ge(low_done, nq - 1)
                nc.vector.tensor_tensor(rem[:, nq % 2, 0:w], bank(jn % 7)[:, 0:w],
                                        dst[:, b, m, 0, n0:n0 + w], ALU.subtract).then_inc(lo_done, 1)
                v.wait_ge(lo_done, nq + 1)
                nc.vector.tensor_copy(dst[:, b, m, 1, n0:n0 + w], rem[:, nq % 2, 0:w]).then_inc(mid_done, 1)
                nq += 1
                if nq >= 2:
                    norm_max(nq - 2)
            norm_max(nq - 1)
            v.wait_ge(norm_done, len(QKJ))
            for b in range(NB):
                for m in range(KT):
                    o = b * 10
                    nc.vector.reduce_max(bnd[:, 0:1], n2[:, o + 2 * m:o + 2 * m + 2], AX.X).then_inc(dve_step, 1)
                    steps[0] += 1
                    seq(nc.vector.reduce_max(bnd[:, 2:3], n2[:, o + 4 + 3 * m:o + 4 + 3 * m + 3], AX.X))
                    seq(nc.vector.tensor_tensor(bnd[:, 4 + 2 * b + m:5 + 2 * b + m], bnd[:, 0:1], bnd[:, 2:3], ALU.mult))
            nc.vector.reduce_max(bnd[:, 0:1], bnd[:, 4:8], AX.X).then_inc(bound_done, 1)
            v.wait_ge(all_max, 1)
            limit = (SAFE / SCALE) ** 2 if not force_shift else -1.0
            nc.vector.tensor_scalar(flag[:, :], bnd[:, 1:2], limit, None, ALU.is_gt).then_inc(flag_done, 1)
            v.wait_ge(flag_done, 1)
            fl = v.value_load(flag[0:1, 0:1], min_val=0, max_val=1)

            def take_maxima(pa, g0, it):
                i = 0
                for r in range(GH):
                    for qt in range(QT):
                        for j, (c0, w) in enumerate(max_pieces(qt)):
                            v.wait_ge(mx_ready, g0 * (GH * NPIECE) + i + 1)
                            nc.vector.reduce_max(mx[:, r, qt, j:j + 1], o_ps[pa][:, 512 * (i % 2):512 * (i % 2) + w],
                                                 AX.X).then_inc(mx_done, 1)
                            i += 1
                v.wait_ge(mx_done, g0 * (GH * NPIECE) + GH * NPIECE + 2)
                nc.vector.tensor_reduce(mrow[:, :, :], mx[:, :, :, :], AX.X, ALU.max, negate=True).then_inc(norm_done, 1)
                v.wait_ge(norm_done, g0 * 3 + len(QKJ) + 1)
                nc.vector.tensor_copy(shift[:, :, :, 0].rearrange("p q h -> p h q"), mrow[:, :, :]).then_inc(norm_done, 1)
                v.wait_ge(norm_done, g0 * 3 + len(QKJ) + 2)
                nc.vector.tensor_tensor(shift[:, :, :, 1].rearrange("p q h -> p h q"), mrow[:, :, :],
                                        shift[:, :, :, 0].rearrange("p q h -> p h q"), ALU.subtract).then_inc(norm_done, 1)
                v.wait_ge(norm_done, g0 * 3 + len(QKJ) + 3)
                nc.vector.sem_inc(sh_done, 1)
                v.wait_ge(shT_ready, g0 + 1)
                nc.vector.tensor_copy(shiftT[:, :], o_ps[pa][0:2 * GH, 0:512].bitcast(BF16)).then_inc(shT_done, 1)

            def masks(g0):
                for s in range(1, NSTEP):
                    for r in range(GH):
                        v.wait_ge(exp_done, (g0 * NSTEP + s) * GH + r + 1 + 2)
                        for (t, q0, c0) in STEPS[s]:
                            w = min(P, S - q0)
                            off = 0
                            if t == 1:
                                w, off = 2 * P - M, M - P
                            a = pbuf[:, s % 2, r, c0:c0 + w]
                            last = nc.vector.scalar_tensor_tensor(a, a, 3.0e38, seen[:, off:off + w], ALU.min, ALU.mult)
                        last.then_inc(mask_done, 1)

            v.wait_ge(zfill, 16 * NS)
            with v.Fori(0, NG) as it:
                for pa in range(2):
                    g0 = it * 2 + pa
                    with v.If(fl > 0):
                        take_maxima(pa, g0, it)
                    masks(g0)
                    v.wait_ge(pv_done, g0 * NSTEP + NSTEP + 2)
                    nc.vector.tensor_copy(
                        oT[:, bass.ds(it // 2, 1), bass.ds((it % 2) * 2 + pa, 1), :].rearrange("p b g n -> p (b g n)"),
                        o_ps[pa]).then_inc(o_free, 1)

            def normalise_heads(t):
                v.wait_ge(ot_ready, t + 1)
                src = bank(t % 2).rearrange("p (g c) -> p g c", c=32)
                if t >= 2:
                    v.wait_ge(ont_ready, t - 1)
                seq(nc.vector.reciprocal(rec[:, t % 2, :], src[:, :, HD]))
                nc.vector.tensor_tensor(on_sb[:, t % 2, :].rearrange("p (h c) -> p h c", c=HD), src[:, :, 0:HD],
                                        rec[:, t % 2, :, None].broadcast_to([P, H, HD]), ALU.mult).then_inc(on_done, 1)

            for t in range(TT + 2):
                if t < TT:
                    normalise_heads(t)
                if t >= 2:
                    v.wait_ge(wo_ready, t - 1)
                    nc.vector.tensor_tensor(xres[:, t - 2, :], xres[:, t - 2, :], bank(4 + t % 2)[:, 0:D], ALU.add).then_inc(x1_done, 1)
                    v.wait_ge(x1_done, t - 1)
                    ins = nc.vector.bn_stats(stats[:, t - 2, :], xres[:, t - 2, :])
            seq(ins)
            for t in range(TT):
                ins = nc.vector.bn_aggr(mv[:, t, :], stats[:, t, :])
            seq(ins)
            normalise(ve2_done, sqrt2_done, xres, xn2_done)
            v.wait_ge(lg_ready, TT)
            lg = bank(6)[:, 0:TE].rearrange("p (t e) -> p t e", e=E)
            pr = r_probs.rearrange("p (t e) -> p t e", e=E)
            seq(nc.vector.reduce_max(r_max, lg, AX.X))
            nc.vector.tensor_tensor(pr, lg, r_max[:, :, None].broadcast_to([P, TT, E]), ALU.subtract).then_inc(lsub_done, 1)
            v.wait_ge(lexp_done, 1)
            seq(nc.vector.reduce_sum(r_max, pr, AX.X))
            seq(nc.vector.reciprocal(r_max, r_max))
            nc.vector.tensor_tensor(pr, pr, r_max[:, :, None].broadcast_to([P, TT, E]), ALU.mult).then_inc(probs_done, 1)
            seq(nc.vector.memset(cand[:, :], 1 << 29))
            seq(nc.vector.memset(r_one, 1.0))
            v.wait_ge(pt_ready, 1)
            seq(nc.vector.tensor_copy(r_PT, bank(0)[:, 0:P]))
            thr = cand[:, 0:1].bitcast(F32)
            for i in range(30):
                bit = 29 - i
                nc.vector.tensor_scalar(r_junk, r_PT, thr, 0.0, ALU.is_ge, ALU.add, accum_out=cnt_b[:, 0:1]).then_inc(cnt_done, 1)
                v.wait_ge(tot_ready, i + 1)
                seq(nc.vector.tensor_scalar(mstep[:, :], bank(1)[:, 0:1], float(CAP) - 0.5, float(1 << bit), ALU.is_lt, ALU.mult))
                if bit:
                    seq(nc.vector.scalar_tensor_tensor(cand[:, :], mstep[:, :], 1 << (bit - 1), cand[:, :],
                                                       ALU.bitwise_or, ALU.bitwise_xor))
                else:
                    seq(nc.vector.tensor_tensor(cand[:, :], mstep[:, :], cand[:, :], ALU.bitwise_xor))
            seq(nc.vector.tensor_scalar(r_junk, r_PT, thr, 0.0, ALU.is_gt, ALU.add, accum_out=cnt_b[:, 1:2]))
            nc.vector.tensor_scalar(r_eq, r_PT, thr, 0.0, ALU.is_equal, ALU.add, accum_out=cnt_b[:, 2:3]).then_inc(cnt_done, 1)
            v.wait_ge(cnt_done, 31)
            seq(nc.vector.tensor_tensor_scan(r_junk, r_one, r_eq, 0.0, ALU.mult, ALU.add))
            v.wait_ge(tot_ready, 31)
            seq(nc.vector.tensor_copy(lim[:, 1:2], bank(2)[:, 0:1]))
            seq(nc.vector.tensor_scalar(lim[:, 0:1], bank(1)[:, 0:1], -1.0, float(CAP), ALU.mult, ALU.add))
            seq(nc.vector.tensor_tensor(lim[:, 0:1], lim[:, 0:1], lim[:, 1:2], ALU.subtract))
            seq(nc.vector.scalar_tensor_tensor(r_eq, r_junk, lim[:, 0:1], r_eq, ALU.is_le, ALU.mult))
            nc.vector.scalar_tensor_tensor(r_sel, r_PT, thr, r_eq, ALU.is_gt, ALU.add).then_inc(sel_done, 1)
            v.wait_ge(selT_ready, 1)
            t3 = r_tmp.rearrange("p (t e) -> p t e", e=E)
            h3 = r_hot.rearrange("p (t e) -> p t e", e=E)
            seq(nc.vector.tensor_copy(r_tmp, bank(0)[:, 0:P]))
            seq(nc.vector.reduce_max(r_any, t3, AX.X))
            seq(nc.vector.tensor_scalar(r_any, r_any, -1.0, 1.0, ALU.mult, ALU.add))
            seq(nc.vector.tensor_tensor(t3, t3, r_any[:, :, None].broadcast_to([P, TT, E]), ALU.add))
            seq(nc.vector.tensor_tensor(h3, t3, pr, ALU.mult))
            seq(nc.vector.scalar_tensor_tensor(r_hot, r_tmp, -1.0, r_hot, ALU.add, ALU.add))
            seq(nc.vector.reduce_max(r_gate, h3, AX.X))
            seq(nc.vector.tensor_tensor(h3, h3, r_gate[:, :, None].broadcast_to([P, TT, E]), ALU.is_equal))
            seq(nc.vector.tensor_scalar(r_e8, fcol[:, 0:E], -1.0, float(E), ALU.mult, ALU.add))
            seq(nc.vector.tensor_tensor(h3, h3, r_e8[:, None, :].broadcast_to([P, TT, E]), ALU.mult))
            seq(nc.vector.reduce_max(r_any, h3, AX.X))
            seq(nc.vector.tensor_tensor(h3, h3, r_any[:, :, None].broadcast_to([P, TT, E]), ALU.is_equal))
            nc.vector.tensor_copy(r_hotb, r_hot).then_inc(hot_done, 1)
            v.wait_ge(hot_done, 1)
            v.wait_ge(rank_ready, 1)
            te3 = r_te.rearrange("p (e t) -> p e t", e=E)
            in3 = r_inc.rearrange("p (e t) -> p e t", e=E)
            seq(nc.vector.tensor_copy(te3, bank(2)[:, 0:TE].rearrange("p (t e) -> p e t", e=E)))
            rs3 = r_reset.rearrange("p (e t) -> p e t", e=E)
            seq(nc.vector.memset(r_reset, 1.0))
            seq(nc.vector.memset(rs3[:, :, 0:1], 0.0))
            seq(nc.vector.tensor_tensor_scan(r_inc, r_reset, r_te, 0.0, ALU.mult, ALU.add))
            seq(nc.vector.tensor_scalar(r_i128, fcol[:, 0:16], float(P), None, ALU.mult))
            jk = r_junk.rearrange("p (e t) -> p e t", e=E)
            seq(nc.vector.tensor_tensor(jk, in3[:, :, TT - 1:TT].broadcast_to([P, E, TT]), r_i128[:, None, :].broadcast_to([P, E, TT]), ALU.is_gt))
            seq(nc.vector.reduce_sum(r_nt, jk, AX.X))
            seq(nc.vector.tensor_tensor_scan(r_end, r_one[:, 0:E], r_nt, 0.0, ALU.mult, ALU.add))
            tx = r_tx.rearrange("p (j e) -> p j e", e=E)
            seq(nc.vector.tensor_tensor(tx, r_end[:, None, :].broadcast_to([P, NS, E]), fcol[:, 0:NS, None].broadcast_to([P, NS, E]), ALU.is_le))
            seq(nc.vector.reduce_sum(r_iota[:, 0:NS], tx, AX.X))
            seq(nc.vector.tensor_scalar(r_texp[:, :], r_iota[:, 0:NS], float(E - 1), None, ALU.min))
            seq(nc.vector.tensor_tensor(in3, in3, te3, ALU.subtract))
            seq(nc.vector.tensor_tensor(r_end, r_end, r_nt, ALU.subtract))
            seq(nc.vector.tensor_scalar(r_end, r_end, float(P), None, ALU.mult))
            seq(nc.vector.tensor_tensor(in3, in3, r_end[:, :, None].broadcast_to([P, E, TT]), ALU.add))
            seq(nc.vector.tensor_tensor(t3, bank(1)[:, 0:TE].rearrange("p (t e) -> p t e", e=E),
                                        r_inc.rearrange("p (e t) -> p t e", e=E), ALU.add))
            seq(nc.vector.tensor_tensor(t3, t3, h3, ALU.mult))
            seq(nc.vector.reduce_sum(r_pos, t3, AX.X))
            nc.vector.tensor_copy(r_posu[:, :], r_pos).then_inc(pos_done, 1)

            def ffn_hT(pa, k):
                v.wait_ge(ft_ready, k + 1 + 2)
                nc.vector.tensor_copy(hT_sb[pa], bank(4 + pa)).then_inc(ft_done, 1)

            def ffn_y(pa, k, stored):
                v.wait_ge(fy_ready, k + 1)
                if stored is not None:
                    v.wait_ge(ys_out[pa], stored)
                nc.vector.tensor_copy(y_sb[pa], bank(6 + pa)[:, 0:D]).then_inc(fy_done, 1)

            for pa in range(2):
                ffn_hT(pa, pa)
                ffn_y(pa, pa, None)
            with v.Fori(1, NS // 2) as it:
                for pa in range(2):
                    ffn_hT(pa, it * 2 + pa)
                    ffn_y(pa, it * 2 + pa, it * 16)
            for t in range(TT):
                v.wait_ge(gath, 16 * TT)
                nc.vector.scalar_tensor_tensor(xres[:, t, :], xn[:, t, :], r_gate[:, t:t + 1], xres[:, t, :],
                                               ALU.mult, ALU.add).then_inc(res_done, 1)


_INS = ["x", "ctx_1024", "L0_xattn_Wq", "L0_xattn_Wkv", "L0_xattn_Wout", "L0_xattn_bout",
        "L0_ffn_Wg", "L0_ffn_W1", "L0_ffn_W2"]
_OUTS = [((NB, S, D), "float32")]


def kernel(**inputs):
    import numpy as _np
    import concourse.bacc as _bacc
    from concourse.bass_utils import run_bass_kernel_spmd as _run

    nc = _bacc.Bacc("TRN2", target_bir_lowering=False, num_devices=1)
    arrays, args = {}, []
    for name in _INS:
        a = _np.ascontiguousarray(inputs[name])
        arrays[f"in_{name}"] = a
        args.append(nc.dram_tensor(f"in_{name}", a.shape, mybir.dt.from_np(a.dtype), kind="ExternalInput").ap())
    for i, (shape, dtype) in enumerate(_OUTS):
        args.append(nc.dram_tensor(f"out_{i}", shape, mybir.dt.from_np(_np.dtype(dtype)), kind="ExternalOutput").ap())
    for name in ("slots_in", "slots_out"):
        args.append(nc.dram_tensor(name, (NS * P, D), F32, kind="Internal").ap())
    xattn_ffn(nc, *args)
    r = _run(nc, [arrays], core_ids=[0])
    return r.results[0]["out_0"]
```

```python
from contextlib import ExitStack

import concourse.bass as bass
from concourse import mybir

F32 = mybir.dt.float32
BF16 = mybir.dt.bfloat16
I32 = mybir.dt.int32
U32 = mybir.dt.uint32
U16 = mybir.dt.uint16
ALU = mybir.AluOpType
ACT = mybir.ActivationFunctionType
AX = mybir.AxisListType

P = 128
NB = 2
S = 1024
M = 154
D = 256
KT = D // P
H = 16
HD = D // H
NG = 4
GH = H // NG
J = M + S
JT = -(-J // P)
JP = JT * P
QT = S // P
T = NB * S
TT = T // P
E = 8
F = 512
FT = F // P
CAP = T // E
NS = (T + E * (P - 1)) // P + 1
SCALE = float(HD) ** -0.5
EPS = 1e-5
NPROD = 6
QPART = [0, 0, 1, 1, 0, 2]
KPART = [0, 1, 0, 1, 2, 0]
LAG = 7
NPIECES = 3
XW = 2 * D
RING = 4
NS = -(-NS // RING) * RING
NS_MOST = (T // P + E // 2) // RING * RING
NOWHERE = 1 << 20
KROWS = NPROD * HD
SROWS = KROWS + 2
VC = 32
SAFE = 40.0
NEG = -1.0e30

def first_query(t):
    return max(0, t * P - M)

STEP_TILES = [[0], [5, 6], [4, 7], [3, 8, 9], [1], [2]]
assert sorted(sum(STEP_TILES, [])) == list(range(JT))
STEPS = []
for _tiles in STEP_TILES:
    _col = first_query(_tiles[0]) if len(_tiles) == 1 else 0
    STEPS.append([])
    for _t in _tiles:
        STEPS[-1].append((_t, first_query(_t), _col))
        _col += S - first_query(_t)
    assert _col <= S
NSTEP = len(STEPS)
def max_pieces(qt):
    width, out = M + P * (qt + 1), []
    while width > 0:
        n = min(512, width)
        out.append((width - n, n))
        width -= n
    return out[::-1]

NPIECE = sum(len(max_pieces(qt)) for qt in range(QT))


def split_at_bank(c0, c1):
    out = []
    while c0 < c1:
        c = min(c1, (c0 // 512 + 1) * 512)
        out.append((c0, c))
        c0 = c
    return out


def halves(pieces):
    cut = min(range(1, len(pieces)), key=lambda i: abs(sum(p[2] - p[1] for p in pieces[:i]) - sum(p[2] - p[1] for p in pieces[i:])))
    return pieces[:cut], pieces[cut:]


VALUE_PIECES = [halves(sorted(((t, a, z, c0 - q0) for (t, q0, c0) in step for (a, z) in split_at_bank(q0, S)),
                              key=lambda p: -p[1])) for step in STEPS]


def xattn_ffn(nc, x, ctx, Wq, Wkv, Wout, bout, Wg, W1, W2, out, rows_d, qd, kd, force_shift=False):
    es = ExitStack()
    with es:
        def sb(name, shape, dt=F32):
            return es.enter_context(nc.sbuf_tensor(name, shape, dt))

        def sem(name):
            return es.enter_context(nc.semaphore(name))

        xres = sb("xres", [P, TT, D])
        wts = sb("wts", [P, E * KT * F + E * FT * D])
        w1_sb = wts[:, 0:E * KT * F]
        w2_sb = wts[:, E * KT * F:]
        VN = NB * JT * D
        v_all = wts[:, E * KT * F + E * FT * D - VN:].rearrange("p (b t n) -> p b t n", b=NB, t=JT)
        E_EARLY = (E * FT * D - VN) // (FT * D)
        piece_f = sb("piece", [P, NPIECES * 3 * 512 // 2])
        piece = piece_f[:, :].bitcast(BF16).rearrange("p (a c n) -> p a c n", a=NPIECES, c=3)
        mx = piece_f[:, 0:GH * QT * 3].rearrange("p (h q j) -> p h q j", h=GH, q=QT)
        c0 = GH * QT * 3
        mrow = piece_f[:, c0:c0 + GH * QT].rearrange("p (h q) -> p h q", h=GH)
        c0 += GH * QT
        shift = piece_f[:, c0:c0 + GH * QT].bitcast(BF16).rearrange("p (q h c) -> p q h c", q=QT, h=GH)
        c0 += GH * QT
        shiftT = piece_f[0:2 * GH, c0:c0 + S // 2].bitcast(BF16)
        mid = sb("mid", [P, NB * NG * S])
        xcT = mid[:, 0:NB * KT * JP].rearrange("p (b k n) -> p b k n", b=NB, k=KT)
        oT = mid[:, :].rearrange("p (b g n) -> p b g n", b=NB, g=NG)
        c0 = NB * KT * JP
        bias = mid[:, c0:c0 + D]
        c0 += D
        icol = mid[:, c0:c0 + P].bitcast(I32)
        ic2 = mid[:, c0 + P:c0 + 2 * P].bitcast(I32)
        q_st = [sb(f"q_st{i}", [SROWS, GH, S], BF16) for i in range(2)]
        k_st = [sb(f"k_st{i}", [SROWS, GH, JP], BF16) for i in range(2)]
        v_st = [sb(f"v_st{i}", [P, JT, GH, VC]) for i in range(2)]
        flat_t = sb("pbuf", [P, TT * XW])
        flat = flat_t[:, :]
        pbuf = flat[:, 0:2 * GH * S].rearrange("p (a h n) -> p a h n", a=2, h=GH)
        xn = flat[:, 0:TT * D].rearrange("p (t n) -> p t n", t=TT)
        rows = flat[:, :].rearrange("p (t n) -> p t n", t=TT)
        ctx_sb = flat[:, TT * D:TT * D + NB * 2 * D].rearrange("p (b t n) -> p b t n", b=NB, t=2)
        WK0 = TT * D
        c0 = WK0 + NB * 2 * D
        wq_sb = flat[:, c0:c0 + KT * D].rearrange("p (k n) -> p k n", k=KT)
        c0 += KT * D
        wkv_sb = flat[:, c0:c0 + KT * 2 * D].rearrange("p (k n) -> p k n", k=KT)
        c0 += KT * 2 * D
        rem = flat[:, c0:c0 + 1024].rearrange("p (a n) -> p a n", a=2)
        c0 += 1024
        sq = flat[:, c0:c0 + 512].bitcast(BF16).rearrange("p (a n) -> p a n", a=2)
        wout_sb = sb("wout_sb", [P, KT, D])
        wg_sb = sb("wg_sb", [P, KT, E])
        ident = sb("ident", [P, P])
        ident_b = sb("ident_b", [P, P], BF16)
        tri = sb("tri", [P, P], BF16)
        heads = sb("heads", [P, P], BF16)
        same_e = sb("same_e", [P, P], BF16)
        prev_e = sb("prev_e", [P, P], BF16)
        before = sb("before", [P, P], BF16)
        ones_b = sb("ones_b", [P, P], BF16)
        seen = sb("seen", [P, P])
        irow = sb("irow", [P, 1], I32)
        ir2 = sb("ir2", [P, 1], I32)
        fcol = sb("fcol", [P, P])
        frow = sb("frow", [P, 4])
        stats = sb("stats", [P, TT, 6])
        mv = sb("mv", [P, TT, 2])
        ve = sb("ve", [P, TT])
        rstd = sb("rstd", [P, TT])
        nt1 = sb("nt1", [P, TT])
        n2 = sb("n2", [P, 20])
        bnd = sb("bnd", [P, 8])
        flag = sb("flag", [P, NB], I32)
        bmax = sb("bmax", [P, NB])
        ball = sb("ball", [P, NB])

        ps = es.enter_context(nc.psum_tensor("ps", [P, 4096], F32))

        def bank(i):
            return ps[:, 512 * i:512 * i + 512]

        st_ps = [ps[:, 0:1024], ps[:, 1024:2048]]
        o_ps = [ps[:, 2048:3072], ps[:, 3072:4096]]

        x_in = [sem(f"x_in{i}") for i in range(4)]
        qk_out = [sem(f"qk_out{i}") for i in range(NPIECES)]
        qk_in = [sem(f"qk_in{i}") for i in range(2)]
        mx_ready = [sem(f"mx_ready{i}") for i in range(2)]
        mx_done = [sem(f"mx_done{i}") for i in range(2)]
        sh_done = [sem(f"sh_done{i}") for i in range(2)]
        shT_ready = [sem(f"shT_ready{i}") for i in range(2)]
        shT_ask = [sem(f"shT_ask{i}") for i in range(2)]
        sh_in = [sem(f"sh_in{i}") for i in range(2)]
        xs_in = [sem(f"xs_in{i}") for i in range(RING)]
        sent = [sem(f"sent{i}") for i in range(RING)]
        ctx_in = sem("ctx_in")
        w_in = sem("w_in")
        w2_small = sem("w2_small")
        bias_in = sem("bias_in")
        ident_made = sem("ident_made")
        iota_made = sem("iota_made")
        st_made = sem("st_made")
        tri_made = sem("tri_made")
        heads_made = sem("heads_made")
        dve_step = sem("dve_step")
        ve_done = sem("ve_done")
        sqrt_done = sem("sqrt_done")
        xn_done = sem("xn_done")
        pad_done = sem("pad_done")
        tr_done = sem("tr_done")
        proj_ready = sem("proj_ready")
        hi_done = sem("hi_done")
        lo_done = sem("lo_done")
        mid_done = sem("mid_done")
        low_done = sem("low_done")
        vcopy_done = sem("vcopy_done")
        sq_done = sem("sq_done")
        norm_ready = sem("norm_ready")
        norm_done = sem("norm_done")
        bound_done = sem("bound_done")
        all_max = sem("all_max")
        flag_done = sem("flag_done")
        ones_rows = sem("ones_rows")
        rows_sent = sem("rows_sent")
        v_in = sem("v_in")
        biased = sem("biased")
        st_ready = sem("st_ready")
        exp_done = sem("exp_done")
        mask_done = sem("mask_done")
        pv_done = sem("pv_done")
        o_free = sem("o_free")
        w1_in = sem("w1_in")
        w2_in = sem("w2_in")
        ot_ready = sem("ot_ready")
        on_done = sem("on_done")
        ont_ready = sem("ont_ready")
        ont_done = sem("ont_done")
        wo_ready = sem("wo_ready")
        x1_done = sem("x1_done")
        ve2_done = sem("ve2_done")
        sqrt2_done = sem("sqrt2_done")
        xn2_done = sem("xn2_done")
        xt2_ready = sem("xt2_ready")
        xt2_done = sem("xt2_done")
        lg_ready = sem("lg_ready")
        lsub_done = sem("lsub_done")
        lexp_done = sem("lexp_done")
        probs_done = sem("probs_done")
        pt_ready = sem("pt_ready")
        cnt_done = sem("cnt_done")
        tot_ready = sem("tot_ready")
        sel_done = sem("sel_done")
        selT_ready = sem("selT_ready")
        hot_done = sem("hot_done")
        rank_ready = sem("rank_ready")
        texp_done = sem("texp_done")
        tile_made = sem("tile_made")
        slots_ready = sem("slots_ready")
        idx_done = sem("idx_done")
        took = sem("took")
        index_there = sem("index_there")
        fx_ready = sem("fx_ready")
        fx_done = sem("fx_done")
        fh_ready = sem("fh_ready")
        fg_done = sem("fg_done")
        fw_done = sem("fw_done")
        fy_ready = sem("fy_ready")
        fy_done = sem("fy_done")

        def jobs_of(b):
            jobs = [("t", b, q4, k) for q4 in range(2) for k in range(KT)] + [("c", b)]
            for m in range(KT):
                jobs += [("q", b, m, n0, 512) for n0 in range(0, S, 512)]
                jobs += [("k", b, m, n0, min(512, J - n0)) for n0 in range(0, J, 512)]
            return jobs + [("v", b, t) for t in range(0, JT, 2)]

        JOBS = jobs_of(0) + jobs_of(1)
        NBK = 7
        QK = [n for n, j in enumerate(JOBS) if j[0] in "qk"]
        TR = [n for n, j in enumerate(JOBS) if j[0] in "tc"]
        VJ = [n for n, j in enumerate(JOBS) if j[0] == "v"]
        PER_HALF = 5
        PER_B = PER_HALF * KT

        def stores(slot, n):
            return len([i for i in range(n) if i % NPIECES == slot])

        work_at = [0]

        def work(n):
            a = mid[:, work_at[0]:work_at[0] + n]
            work_at[0] += n
            assert work_at[0] <= NB * NG * S
            return a

        xs_sb = [work(XW) for _ in range(RING)]
        y_sb = [work(D) for _ in range(RING)]
        xT_sb = [work(D) for _ in range(2)]
        hT_sb = [work(F) for _ in range(2)]
        in_tile = [work(P) for _ in range(RING)]
        of_tile = work(TT * NS).rearrange("p (t n) -> p t n", t=TT)
        hv = work(TT * 2 * NS).rearrange("p (t c n) -> p t c n", t=TT, c=2)
        on_sb = piece_f[:, 0:2 * D].rearrange("p (a n) -> p a n", a=2)
        onT_sb = piece_f[:, 2 * D:4 * D].rearrange("p (a n) -> p a n", a=2)
        xt2_sb = piece_f[:, 4 * D:6 * D].rearrange("p (a n) -> p a n", a=2)

        w1c_sb = [piece_f[:, i * KT * F:(i + 1) * KT * F] for i in range(2)]

        TE = TT * E
        route = [[v_st[i][:, :, :, :].rearrange("p t h c -> p (t h c)"), 0] for i in range(2)]

        def rwork(i, n):
            buf, at = route[i]
            route[i][1] += n
            assert route[i][1] <= JT * GH * VC
            return buf[:, at:at + n]

        r_probs = rwork(0, TE)
        r_max = rwork(0, TT)
        r_PT = rwork(0, P)
        r_junk = rwork(0, P)
        r_eq = rwork(0, P)
        r_sel = rwork(0, P)
        r_one = rwork(0, P)
        r_tmp = rwork(0, TE)
        r_hot = rwork(0, TE)
        r_te = rwork(1, TE)
        r_inc = rwork(1, TE)
        r_reset = rwork(1, TE)
        r_exp = rwork(1, NS)
        r_i128 = rwork(1, 16)
        r_e8 = rwork(1, E)
        r_nt = rwork(1, E)
        r_end = rwork(1, E)
        r_pos = rwork(1, TT)
        r_any = rwork(1, TT)
        r_gate = rwork(1, TT)
        r_tx = rwork(1, NS * E)
        r_ge = [rwork(1, P // 2).bitcast(U16) for _ in range(3)]
        r_key = [rwork(0, P // 2).bitcast(U16) for _ in range(2)]
        r_low = rwork(1, P)
        r_int = rwork(1, P).bitcast(I32)
        r_hotb = rwork(1, TE // 2).bitcast(BF16)
        r_posi = sb("r_posi", [P, 2, TT], I32)
        r_posf = sb("r_posf", [P, 2, TT])
        tok1 = sb("tok1", [P, TT])
        slot_tok = sb("slot_tok", [P, NS], U32)
        slot_gate = sb("slot_gate", [P, NS])
        nowhere = sb("nowhere", [P, NS])
        more = sb("more", [P, 1], I32)
        take_ix = [sb(f"take_ix{i}", [P, 1], U32) for i in range(RING)]
        give_ix = [sb(f"give_ix{i}", [P, 1], U32) for i in range(RING)]
        zero1 = sb("zero1", [P, 1], U32)
        r_texp = sb("r_texp", [P, NS], I32)
        LOW = 14
        SHIFTS = [list(range(14, -1, -2)), list(range(LOW - 2, -1, -2))]
        ROUNDS = len(SHIFTS[0]) + len(SHIFTS[1])
        jint = sb("jint", [P, 4], I32)
        digit = sb("digit", [P, ROUNDS, 4])
        cand = sb("cand", [P, 4])
        nxt = sb("nxt", [P, 4])
        ndig = sb("ndig", [P, 4])
        cnt_b = sb("cnt_b", [P, 4], BF16)
        lim = sb("lim", [P, 2])
        warm = sb("warm", [1, 1])
        rec = sb("rec", [P, 2, H])
        tok = sb("tok", [P, TT], I32)
        slot_no = sb("slot_no", [P, NS], I32)

        def xt2_bank(t):
            return 0 if t + LAG >= TT + 2 and t % 2 else 6

        blk = es.enter_context(nc.Block())

        @blk.sync
        def _(sp):
            xr = x.rearrange("b (t p) d -> p (b t) d", p=P)
            n = TT // 4
            for i in range(4):
                sp.dma_start(xres[:, i * n:(i + 1) * n, :], xr[:, i * n:(i + 1) * n, :]).then_inc(x_in[i], 16)
                if i == 1:
                    sp.dma_start(wq_sb[:, :, :], Wq.rearrange("(k p) n -> p k n", p=P)).then_inc(w_in, 16)
                    sp.dma_start(wkv_sb[:, :, :], Wkv.rearrange("(k p) n -> p k n", p=P)).then_inc(w_in, 16)
            sp.dma_start(wout_sb[:, :, :], Wout.rearrange("(k p) n -> p k n", p=P)).then_inc(w2_small, 16)
            sp.dma_start(wg_sb[:, :, :], Wg.rearrange("(k p) n -> p k n", p=P)).then_inc(w2_small, 16)
            sp.dma_start(bias[:, :], bout.partition_broadcast(P)).then_inc(bias_in, 16)

            def store_pieces(i0, i1):
                for i in range(i0, i1):
                    kind, b, m, n0, w = JOBS[QK[i]]
                    sp.wait_ge(mid_done, i + 1)
                    sp.wait_ge(low_done, i + 1)
                    dst = (qd if kind == "q" else kd)[b, m, :, :, n0:n0 + w]
                    sp.dma_start(dst.rearrange("c p n -> p c n"), piece[:, i % NPIECES, :, 0:w]).then_inc(qk_out[i % NPIECES], 16)

            def stage(pa, b, m):
                for c in range(NPROD):
                    for st, src, part, w in ((q_st, qd, QPART, S), (k_st, kd, KPART, J)):
                        sp.dma_start(st[pa][HD * c:HD * c + HD, :, 0:w],
                                     src[bass.ds(b, 1), bass.ds(m, 1), part[c], GH * HD * pa:GH * HD * (pa + 1), :]
                                     .rearrange("b m (r d) n -> d (b m r) n", d=HD)).then_inc(qk_in[pa], 16)

            store_pieces(0, PER_B)
            sp.wait_ge(ones_rows, 2)
            for i in range(NPIECES):
                sp.wait_ge(qk_out[i], 16 * stores(i, PER_B))
            for pa in range(2):
                stage(pa, 0, 0)
            store_pieces(PER_B, 2 * PER_B)
            for e in range(E):
                sp.dma_start(w1_sb[:, e * KT * F:(e + 1) * KT * F].rearrange("p (k n) -> p k n", k=KT),
                             W1[e].rearrange("(k p) n -> p k n", p=P)).then_inc(w1_in, 16)
                if e < E_EARLY:
                    sp.dma_start(w2_sb[:, e * FT * D:(e + 1) * FT * D].rearrange("p (k n) -> p k n", k=FT),
                                 W2[e].rearrange("(k p) n -> p k n", p=P)).then_inc(w2_in, 16)
            for i in range(NPIECES):
                sp.wait_ge(qk_out[i], 16 * stores(i, 2 * PER_B))

            def shift_rows(pa, g0):
                sp.wait_ge(flag_done, g0 // (2 * KT) + 1)
                fl = sp.value_load(flag[0:1, bass.ds(g0 // (2 * KT), 1)], min_val=0, max_val=1)
                with sp.If(fl > 0):
                    sp.wait_ge(shT_ask[pa], g0 // 2 + 1)
                    for r in range(GH):
                        sp.dma_start(q_st[pa][KROWS:SROWS, r, :], shiftT[2 * r:2 * r + 2, :]).then_inc(sh_in[pa], 16)

            shift_rows(0, 0)
            with sp.Fori(0, NG - 1) as it:
                shift_rows(1, it * 2 + 1)
                sp.wait_ge(pv_done, it * (2 * NSTEP) + NSTEP + 2)
                stage(0, (it + 1) // 2, (it + 1) % 2)
                shift_rows(0, it * 2 + 2)
                sp.wait_ge(pv_done, it * (2 * NSTEP) + 2 * NSTEP + 2)
                stage(1, (it + 1) // 2, (it + 1) % 2)
            shift_rows(1, 2 * NG - 1)
            sp.wait_ge(v_in, 2 * NG)
            for e in range(E_EARLY, E):
                sp.dma_start(w2_sb[:, e * FT * D:(e + 1) * FT * D].rearrange("p (k n) -> p k n", k=FT),
                             W2[e].rearrange("(k p) n -> p k n", p=P)).then_inc(w2_in, 16)
            for c in range(TT // 4):
                sp.wait_ge(xn2_done, 4 * c + 4)
                sp.dma_start(rows_d.rearrange("(t p) n -> p t n", p=P)[:, 4 * c:4 * c + 4, :],
                             rows[:, 4 * c:4 * c + 4, :]).then_inc(rows_sent, 16)
            for u in range(RING):
                sp.wait_ge(sent[u], 16 * (NS_MOST // RING))
            sp.wait_ge(texp_done, 2)
            fl = sp.value_load(more[0:1, 0:1], min_val=0, max_val=1)
            with sp.If(fl > 0):
                for u in range(RING):
                    sp.wait_ge(sent[u], 16 * (NS // RING))

        @blk.gpsimd
        def _(pool):
            pool.dma_start(ctx_sb[:, :, 0, :], ctx[:, 0:P, :].rearrange("b p d -> p b d")).then_inc(ctx_in, 16)
            pool.dma_start(ctx_sb[0:M - P, :, 1, :], ctx[:, P:M, :].rearrange("b p d -> p b d")).then_inc(ctx_in, 16)
            nc.gpsimd.memset(ident[:, :], 0.0).then_inc(ident_made, 1)
            pool.wait_ge(ident_made, 1)
            nc.gpsimd.affine_select(out=ident[:, :], in_=ident[:, :], compare_op=ALU.not_equal, fill=1.0,
                                    base=0, pattern=[[-1, P]], channel_multiplier=1).then_inc(ident_made, 1)
            nc.gpsimd.iota(icol, pattern=[[1, P]], base=0, channel_multiplier=0).then_inc(iota_made, 1)
            nc.gpsimd.iota(irow[:, :], pattern=[[0, 1]], base=0, channel_multiplier=1).then_inc(iota_made, 1)
            nc.gpsimd.iota(jint[:, :], pattern=[[1, 4]], base=0, channel_multiplier=0).then_inc(iota_made, 1)
            nc.gpsimd.iota(tok[:, :], pattern=[[P, TT]], base=1, channel_multiplier=1).then_inc(iota_made, 1)
            nc.gpsimd.iota(slot_no[:, :], pattern=[[P, NS]], base=NOWHERE, channel_multiplier=1).then_inc(iota_made, 1)
            made = 0
            for i in range(2):
                nc.gpsimd.memset(v_st[i][:, :, :, :], 0.0).then_inc(st_made, 1)
                nc.gpsimd.memset(k_st[i][:, :, J:JP].bitcast(F32), 0.0).then_inc(st_made, 1)
                made += 2
                pool.wait_ge(st_made, made)
            for i in range(2):
                nc.gpsimd.memset(q_st[i][KROWS:SROWS, :, :].rearrange("p h n -> p (h n)").bitcast(F32), 0.0).then_inc(st_made, 1)
                made += 1
                pool.wait_ge(st_made, made)
                nc.gpsimd.memset(k_st[i][KROWS:SROWS, :, 0:J], 1.0).then_inc(ones_rows, 1)
                pool.wait_ge(ones_rows, i + 1)
            for i in range(2):
                nc.gpsimd.memset(v_st[i][:, 0:JT - 1, :, HD:HD + 1], 1.0).then_inc(st_made, 1)
                made += 1
            pool.wait_ge(st_made, made)
            for i in range(2):
                nc.gpsimd.memset(v_st[i][0:J - (JT - 1) * P, JT - 1, :, HD:HD + 1], 1.0).then_inc(st_made, 1)
                made += 1
            pool.wait_ge(st_made, made)
            nc.gpsimd.memset(tri[:, :], 0.0).then_inc(tri_made, 1)
            pool.wait_ge(tri_made, 1)
            nc.gpsimd.affine_select(out=tri[:, :], in_=tri[:, :], compare_op=ALU.is_ge, fill=NEG,
                                    base=0, pattern=[[-1, P]], channel_multiplier=1).then_inc(tri_made, 1)
            nc.gpsimd.memset(zero1[:, :], 0).then_inc(tri_made, 1)

            def over_partitions(b):
                pool.wait_ge(bound_done, b + 1)
                nc.gpsimd.partition_all_reduce(ball[:, b:b + 1], bmax[:, b:b + 1], P, bass.bass_isa.ReduceOp.max).then_inc(all_max, 1)

            def load_v(pa, b, m):
                g = 2 * m + pa
                nc.gpsimd.tensor_copy(v_st[pa][:, :, :, 0:HD],
                                      v_all[:, bass.ds(b, 1), :, bass.ds(g * (GH * HD), GH * HD)]
                                      .rearrange("p b t (h c) -> p (b t) h c", h=GH)).then_inc(v_in, 1)

            for i in range(len(QK)):
                w = JOBS[QK[i]][4]
                if i == PER_B:
                    pool.wait_ge(bias_in, 16)
                    pool.wait_ge(xn_done, TT)
                    for t in range(TT):
                        nc.gpsimd.tensor_tensor(xres[:, t, :], xres[:, t, :], bias, ALU.add).then_inc(biased, 1)
                    pool.wait_ge(vcopy_done, len(VJ) // 2)
                    for pa in range(2):
                        load_v(pa, 0, 0)
                pool.wait_ge(mid_done, i + 1)
                nc.gpsimd.tensor_tensor(piece[:, i % NPIECES, 2, 0:w], rem[:, i % 2, 0:w],
                                        piece[:, i % NPIECES, 1, 0:w], ALU.subtract).then_inc(low_done, 1)
                if i == PER_B + 2:
                    over_partitions(0)
            over_partitions(1)

            pool.wait_ge(vcopy_done, len(VJ))
            with pool.Fori(0, NG - 1) as it:
                for pa in range(2):
                    pool.wait_ge(pv_done, it * (2 * NSTEP) + NSTEP * (pa + 1) + 2)
                    load_v(pa, (it + 1) // 2, (it + 1) % 2)
            pool.wait_ge(idx_done, 2)
            pool.wait_ge(rows_sent, 16 * (TT // 4))
            pool.wait_ge(ot_ready, TT)

            def take(u, k, at):
                nc.gpsimd.tensor_tensor(take_ix[u][:, :], slot_tok[:, bass.ds(k, 1)], zero1[:, :], ALU.add).then_inc(took, 1)
                pool.wait_ge(took, at)
                pool.sem_inc(index_there, 1)
                pool.indirect_dma_start(xs_sb[u], None, rows_d[:, :], bass.IndirectOffsetOnAxis(take_ix[u][:, :], 0),
                                        bounds_check=T - 1, oob_is_err=False).then_inc(xs_in[u], 16)

            out_rows = out.rearrange("b s d -> (b s) d")

            def give(u, k, at):
                pool.wait_ge(fy_done, k + 1 + 2)
                nc.gpsimd.tensor_tensor(give_ix[u][:, :], slot_tok[:, bass.ds(k, 1)], zero1[:, :], ALU.add).then_inc(took, 1)
                pool.wait_ge(took, at)
                pool.sem_inc(index_there, 1)
                pool.indirect_dma_start(out_rows, bass.IndirectOffsetOnAxis(give_ix[u][:, :], 0), y_sb[u], None,
                                        bounds_check=T - 1, oob_is_err=False).then_inc(sent[u], 16)

            for u in range(RING):
                take(u, u, u + 1)
            for u in range(RING):
                pool.wait_ge(fy_done, u + 1 + 2)
                take(u, RING + u, RING + 2 * u + 1)
                give(u, u, RING + 2 * u + 2)
            with pool.Fori(1, NS_MOST // RING - 1) as it:
                for u in range(RING):
                    pool.wait_ge(fy_done, it * RING + u + 1 + 2)
                    take(u, it * RING + RING + u, it * (2 * RING) + RING + 2 * u + 1)
                    pool.wait_ge(sent[u], it * 16)
                    give(u, it * RING + u, it * (2 * RING) + RING + 2 * u + 2)
            at = 2 * NS_MOST - RING
            for u in range(RING):
                pool.wait_ge(sent[u], 16 * (NS_MOST // RING - 1))
                give(u, NS_MOST - RING + u, at + u + 1)
            pool.wait_ge(texp_done, 2)
            fl = pool.value_load(more[0:1, 0:1], min_val=0, max_val=1)
            with pool.If(fl > 0):
                with pool.Fori(NS_MOST // RING, NS // RING) as it:
                    for u in range(RING):
                        take(u, it * RING + u, it * (2 * RING) + u + 1)
                    for u in range(RING):
                        pool.wait_ge(sent[u], it * 16)
                        give(u, it * RING + u, it * (2 * RING) + RING + u + 1)

        @blk.scalar
        def _(act):
            def root(c):
                act.wait_ge(ve_done, c + 1)
                nc.scalar.activation(rstd[:, 4 * c:4 * c + 4], ve[:, 4 * c:4 * c + 4], ACT.Sqrt).then_inc(sqrt_done, 1)

            root(0)
            root(1)
            nqk = 0
            for jn, job in enumerate(JOBS):
                act.wait_ge(proj_ready, jn + 1)
                bk, b = bank(jn % NBK), job[1]
                if job[0] == "t":
                    q4, k = job[2], job[3]
                    nc.scalar.copy(xcT[:, b, k, M + 512 * q4:M + 512 * q4 + 512], bk).then_inc(tr_done, 1)
                elif job[0] == "c":
                    nc.scalar.copy(xcT[:, b, :, 0:M], bk[:, 0:KT * M].rearrange("p (k n) -> p k n", k=KT)).then_inc(tr_done, 1)
                    if b == 0:
                        root(2)
                        root(3)
                elif job[0] == "v":
                    nc.scalar.copy(v_all[:, b, job[2]:job[2] + 2, :], bk.rearrange("p (t n) -> p t n", t=2)).then_inc(vcopy_done, 1)
                else:
                    w, sl = job[4], nqk % NPIECES
                    if nqk >= NPIECES:
                        act.wait_ge(qk_out[sl], 16 * (nqk // NPIECES))
                    nc.scalar.copy(piece[:, sl, 0, 0:w], bk[:, 0:w]).then_inc(hi_done, 1)
                    if nqk >= 2:
                        act.wait_ge(norm_ready, nqk - 1)
                    nc.scalar.activation(sq[:, nqk % 2, 0:w], bk[:, 0:w], ACT.Square).then_inc(sq_done, 1)
                    nqk += 1

            def exps(g0):
                for s in range(NSTEP):
                    c0 = STEPS[s][0][2]
                    c1 = STEPS[s][-1][2] + S - STEPS[s][-1][1]
                    for r in range(GH):
                        act.wait_ge(st_ready, (g0 * NSTEP + s) * GH + r + 1)
                        if r == 0:
                            act.wait_ge(pv_done, g0 * NSTEP + s + 1)
                        nc.scalar.activation(pbuf[:, s % 2, r, c0:c1], st_ps[r % 2][:, c0:c1], ACT.Exp,
                                             scale=SCALE).then_inc(exp_done, 1)

            nc.scalar.activation(warm[:, :], rstd[0:1, 0:1], ACT.Exp)
            with act.Fori(0, NG) as it:
                for pa in range(2):
                    exps(it * 2 + pa)

            for t in range(TT + LAG + 1):
                if t >= 1 and t <= TT:
                    act.wait_ge(ont_ready, t)
                    if t >= 3:
                        act.wait_ge(wo_ready, t - 2)
                    nc.scalar.copy(onT_sb[:, (t - 1) % 2, :], bank(2 + (t - 1) % 2)[:, 0:D]).then_inc(ont_done, 1)
                if t >= 2 and (t - 2) % 4 == 3 and t - 2 < TT:
                    c = (t - 2) // 4
                    act.wait_ge(ve2_done, c + 1)
                    nc.scalar.activation(rstd[:, 4 * c:4 * c + 4], ve[:, 4 * c:4 * c + 4], ACT.Sqrt).then_inc(sqrt2_done, 1)
                u = t - LAG
                if 0 <= u < TT:
                    act.wait_ge(xt2_ready, u + 1)
                    if u >= 2:
                        act.wait_ge(lg_ready, u - 1)
                    nc.scalar.copy(xt2_sb[:, u % 2, :], bank(xt2_bank(u))[:, 0:D]).then_inc(xt2_done, 1)
            act.wait_ge(lsub_done, 1)
            nc.scalar.activation(r_probs, r_probs, ACT.Exp).then_inc(lexp_done, 1)

            act.sem_inc(fx_done, 2)
            act.sem_inc(fg_done, 2)
            nc.scalar.activation(warm[:, :], rstd[0:1, 0:1], ACT.Gelu)
            act.wait_ge(texp_done, 2)
            act.wait_ge(w1_in, 16 * E)

            def ffn_w(pa, k):
                e = act.value_load(r_texp[0:1, bass.ds(k, 1)], min_val=0, max_val=E - 1)
                act.wait_ge(fh_ready, k + 1)
                nc.scalar.copy(w1c_sb[pa], w1_sb[:, bass.ds(e * (KT * F), KT * F)]).then_inc(fw_done, 1)

            def ffn_x(pa, k):
                act.wait_ge(fx_ready, k + 1)
                act.wait_ge(fh_ready, k + 1)
                nc.scalar.copy(xT_sb[pa], bank(pa)[:, 0:D]).then_inc(fx_done, 1)

            def ffn_h(pa, k):
                act.wait_ge(fh_ready, k + 1 + 2)
                act.wait_ge(fy_ready, k + 1)
                nc.scalar.activation(hT_sb[pa], bank(2 + pa), ACT.Gelu).then_inc(fg_done, 1)

            def tiles(k, last):
                for u in range(RING):
                    nxt = u < RING - 1 or not last
                    if nxt:
                        ffn_w((u + 1) % 2, k + u + 1)
                    ffn_h(u % 2, k + u)
                    if nxt:
                        ffn_x((u + 1) % 2, k + u + 1)

            ffn_w(0, 0)
            ffn_x(0, 0)
            with act.Fori(0, NS_MOST // RING - 1) as it:
                tiles(it * RING, False)
            tiles(NS_MOST - RING, True)
            fl = act.value_load(more[0:1, 0:1], min_val=0, max_val=1)
            with act.If(fl > 0):
                with act.Fori(NS_MOST // RING, NS // RING) as it:
                    ffn_w(0, it * RING)
                    ffn_x(0, it * RING)
                    tiles(it * RING, True)

        @blk.tensor
        def _(pe):
            pe.sem_inc(exp_done, 2)
            pe.sem_inc(pv_done, 2)
            pe.sem_inc(fh_ready, 2)
            pe.sem_inc(fy_ready, 2)

            def norms(i):
                w = JOBS[QK[i]][4]
                pe.wait_ge(sq_done, i + 1)
                if i >= 1:
                    pe.wait_ge(norm_done, i)
                nc.tensor.matmul(bank(7)[:, 0:w], heads[:, :], sq[:, i % 2, 0:w], start=True, stop=True).then_inc(norm_ready, 1)

            normed = 0
            for jn, job in enumerate(JOBS):
                prev, b = jn - NBK, job[1]
                bk = bank(jn % NBK)
                if prev >= 0:
                    if prev in VJ:
                        pe.wait_ge(vcopy_done, VJ.index(prev) + 1)
                    elif prev in TR:
                        pe.wait_ge(tr_done, TR.index(prev) + 1)
                    else:
                        pe.wait_ge(lo_done, QK.index(prev) + 1)
                if job[0] == "t":
                    q4, k = job[2], job[3]
                    if jn == 0:
                        pe.wait_ge(ident_made, 2)
                    pe.wait_ge(xn_done, b * QT + 4 * q4 + 4)
                    for i in range(4):
                        last = nc.tensor.transpose(bk[:, i * P:(i + 1) * P],
                                                   xn[:, b * QT + 4 * q4 + i, k * P:(k + 1) * P], ident[:, :])
                elif job[0] == "c":
                    pe.wait_ge(ctx_in, 32)
                    for k in range(KT):
                        nc.tensor.transpose(bk[:, k * M:k * M + P], ctx_sb[:, b, 0, k * P:(k + 1) * P], ident[:, :])
                        last = nc.tensor.transpose(bk[:, k * M + P:k * M + M],
                                                   ctx_sb[0:M - P, b, 1, k * P:(k + 1) * P], ident[0:M - P, 0:M - P])
                elif job[0] == "v":
                    t = job[2]
                    pe.wait_ge(pad_done, 1)
                    for i in range(2):
                        for k in range(KT):
                            last = nc.tensor.matmul(bk[:, i * D:(i + 1) * D], xcT[:, b, k, (t + i) * P:(t + i + 1) * P],
                                                    wkv_sb[:, k, D:2 * D], start=(k == 0), stop=(k == KT - 1))
                else:
                    m, n0, w = job[2:]
                    pe.wait_ge(w_in, 32)
                    pe.wait_ge(tr_done, len(TR) // 2 * (b + 1))
                    for k in range(KT):
                        w_ap = (wq_sb if job[0] == "q" else wkv_sb)[:, k, m * P:(m + 1) * P]
                        c0 = n0 + (M if job[0] == "q" else 0)
                        last = nc.tensor.matmul(bk[:, 0:w], w_ap, xcT[:, b, k, c0:c0 + w],
                                                start=(k == 0), stop=(k == KT - 1))
                last.then_inc(proj_ready, 1)
                while normed < len(QK) and QK[normed] <= jn - 2:
                    if normed == 0:
                        pe.wait_ge(heads_made, 1)
                    norms(normed)
                    normed += 1
            pe.wait_ge(vcopy_done, len(VJ))
            pe.wait_ge(lo_done, len(QK))
            pe.wait_ge(norm_done, len(QK))
            pe.wait_ge(low_done, len(QK))

            def scores(pa, s, r, g0):
                pe.wait_ge(exp_done, (g0 * NSTEP + s) * GH + r + 1)
                for (t, q0, c0) in STEPS[s]:
                    for (a, z) in split_at_bank(c0, c0 + S - q0):
                        last = nc.tensor.matmul(st_ps[r % 2][:, a:z], k_st[pa][:, r, t * P:(t + 1) * P],
                                                q_st[pa][:, r, q0 + a - c0:q0 + z - c0], start=True, stop=True)
                last.then_inc(st_ready, 1)

            def values(pa, s, g0, half):
                pieces = VALUE_PIECES[s][half]
                if s == 0:
                    pe.wait_ge(o_free, g0 + 1)
                    pe.wait_ge(v_in, g0 + 1)
                    pe.wait_ge(exp_done, (g0 * NSTEP + s) * GH + GH + 2)
                else:
                    pe.wait_ge(mask_done, g0 * ((NSTEP - 1) * GH) + s * GH)
                for (t, a, z, dc) in pieces:
                    for r in range(GH):
                        last = nc.tensor.matmul(o_ps[pa][32 * r:32 * r + 32, a:z], v_st[pa][:, t, r, :],
                                                pbuf[:, s % 2, r, a + dc:z + dc],
                                                start=(t == 0), stop=(t == STEP_TILES[-1][-1]), skip_group_check=True)
                if half == 1:
                    last.then_inc(pv_done, 1)

            def maxima(pa, g0):
                pe.wait_ge(o_free, g0 + 1)
                i = 0
                for r in range(GH):
                    for qt in range(QT):
                        for (c0, w) in max_pieces(qt):
                            pe.wait_ge(mx_done[pa], (g0 // 2) * (GH * NPIECE) + i + 1)
                            b0 = o_ps[pa][:, 512 * (i % 2):512 * (i % 2) + w]
                            last = nc.tensor.matmul(b0, q_st[pa][0:KROWS, r, qt * P:(qt + 1) * P],
                                                    k_st[pa][0:KROWS, r, c0:c0 + w], start=True, stop=True, skip_group_check=True)
                            if c0 + w == M + P * (qt + 1):
                                last = nc.tensor.matmul(b0[:, w - P:w], ident_b[:, :], tri[:, :], start=False, stop=True,
                                                        skip_group_check=True)
                            last.then_inc(mx_ready[pa], 1)
                            i += 1
                pe.wait_ge(sh_done[pa], g0 // 2 * 3 + 3)
                bt = o_ps[pa][0:2 * GH, 0:512].bitcast(BF16)
                for qt in range(QT):
                    last = nc.tensor.transpose(bt[:, qt * P:(qt + 1) * P],
                                               shift[:, qt, :, :].rearrange("p h c -> p (h c)"), ident_b[:, :])
                last.then_inc(shT_ready[pa], 1)
                pe.wait_ge(sh_in[pa], g0 // 2 * (16 * GH) + 16 * GH)

            def values_before(half, pa, s, g0, before_g):
                if s > 0:
                    values(pa, s - 1, g0, half)
                elif before_g is not None:
                    values(1 - pa, NSTEP - 1, before_g, half)

            def group(pa, g0, before_g=None):
                pe.wait_ge(qk_in[pa], g0 // 2 * (16 * 2 * NPROD) + 16 * 2 * NPROD)
                pe.wait_ge(flag_done, g0 // (2 * KT) + 1)
                fl = pe.value_load(flag[0:1, bass.ds(g0 // (2 * KT), 1)], min_val=0, max_val=1)
                with pe.If(fl > 0):
                    maxima(pa, g0)
                for s in range(NSTEP):
                    scores(pa, s, 0, g0)
                    scores(pa, s, 1, g0)
                    values_before(0, pa, s, g0, before_g)
                    scores(pa, s, 2, g0)
                    scores(pa, s, 3, g0)
                    values_before(1, pa, s, g0, before_g)

            group(0, 0)
            with pe.Fori(0, NG - 1) as it:
                group(1, it * 2 + 1, it * 2)
                group(0, it * 2 + 2, it * 2 + 1)
            group(1, 2 * NG - 1, 2 * NG - 2)
            for half in range(2):
                values(1, NSTEP - 1, 2 * NG - 1, half)
            pe.wait_ge(o_free, 2 * NG + 2)
            pe.wait_ge(w2_small, 32)

            def rows_out(t):
                if t >= 2:
                    pe.wait_ge(on_done, t - 1)
                for g in range(NG):
                    last = nc.tensor.transpose(bank(t % 2)[:, g * P:(g + 1) * P],
                                               oT[:, t // QT, g, (t % QT) * P:(t % QT + 1) * P], ident[:, :])
                last.then_inc(ot_ready, 1)

            def back(t):
                pe.wait_ge(on_done, t + 1)
                if t >= 2:
                    pe.wait_ge(ont_done, t - 1)
                for k in range(KT):
                    last = nc.tensor.transpose(bank(2 + t % 2)[:, k * P:(k + 1) * P], on_sb[:, t % 2, k * P:(k + 1) * P], ident[:, :])
                last.then_inc(ont_ready, 1)

            def wout(t):
                pe.wait_ge(ont_done, t + 1)
                if t >= 2:
                    pe.wait_ge(x1_done, t - 1)
                for k in range(KT):
                    last = nc.tensor.matmul(bank(4 + t % 2)[:, 0:D], onT_sb[:, t % 2, k * P:(k + 1) * P], wout_sb[:, k, :],
                                            start=(k == 0), stop=(k == KT - 1))
                last.then_inc(wo_ready, 1)

            def xt2(t):
                pe.wait_ge(xn2_done, t + 1)
                same = [u for u in range(t) if xt2_bank(u) == xt2_bank(t)]
                if same:
                    pe.wait_ge(xt2_done, same[-1] + 1)
                for k in range(KT):
                    last = nc.tensor.transpose(bank(xt2_bank(t))[:, k * P:(k + 1) * P], rows[:, t, k * P:(k + 1) * P], ident[:, :])
                last.then_inc(xt2_ready, 1)

            def logits(t):
                pe.wait_ge(xt2_done, t + 1)
                for k in range(KT):
                    last = nc.tensor.matmul(bank(7)[:, t * E:(t + 1) * E], xt2_sb[:, t % 2, k * P:(k + 1) * P], wg_sb[:, k, :],
                                            start=(k == 0), stop=(k == KT - 1))
                last.then_inc(lg_ready, 1)

            for t in range(TT + LAG + 1):
                if t < TT:
                    rows_out(t)
                if 1 <= t <= TT:
                    back(t - 1)
                if 2 <= t <= TT + 1:
                    wout(t - 2)
                if 0 <= t - LAG < TT:
                    xt2(t - LAG)
                if 0 <= t - LAG - 1 < TT:
                    logits(t - LAG - 1)
            pe.wait_ge(probs_done, 1)
            nc.tensor.transpose(bank(0)[:, 0:P], r_probs, ident[:, :]).then_inc(pt_ready, 1)
            for i in range(ROUNDS):
                pe.wait_ge(cnt_done, i + 1)
                nc.tensor.matmul(bank(1)[:, 0:3], same_e[:, :], cnt_b[:, 0:3], start=True, stop=True).then_inc(tot_ready, 1)
            pe.wait_ge(cnt_done, ROUNDS + 1)
            nc.tensor.matmul(bank(1)[:, 0:1], same_e[:, :], cnt_b[:, 0:1], start=True, stop=True)
            nc.tensor.matmul(bank(2)[:, 0:1], prev_e[:, :], cnt_b[:, 1:2], start=True, stop=True).then_inc(tot_ready, 1)
            pe.wait_ge(sel_done, 1)
            nc.tensor.transpose(bank(0)[:, 0:P], r_sel, ident[:, :]).then_inc(selT_ready, 1)
            pe.wait_ge(hot_done, 1)
            nc.tensor.matmul(bank(1)[:, 0:TE], before[:, :], r_hotb, start=True, stop=True)
            nc.tensor.matmul(bank(2)[:, 0:TE], ones_b[:, :], r_hotb, start=True, stop=True).then_inc(rank_ready, 1)

            for t in range(TT):
                pe.wait_ge(tile_made, t + 1)
                last = nc.tensor.matmul(bank(3)[:, 0:2 * NS], in_tile[t % RING], hv[:, t, :, :].rearrange("p c n -> p (c n)"),
                                        start=(t == 0), stop=(t == TT - 1)).then_inc(slots_ready, 1)

            def ffn_xt(u, k, nth):
                pa = u % 2
                pe.wait_ge(xs_in[u], nth)
                pe.wait_ge(fx_done, k + 1)
                for kk in range(KT):
                    last = nc.tensor.transpose(bank(pa)[:, kk * P:(kk + 1) * P], xs_sb[u][:, kk * P:(kk + 1) * P], ident[:, :])
                last.then_inc(fx_ready, 1)

            def ffn_w1(pa, k):
                pe.wait_ge(fw_done, k + 1)
                pe.wait_ge(fx_done, k + 1 + 2)
                pe.wait_ge(fg_done, k + 1)
                for c in range(FT):
                    for kk in range(KT):
                        last = nc.tensor.matmul(bank(2 + pa)[:, c * P:(c + 1) * P],
                                                w1c_sb[pa][:, kk * F + c * P:kk * F + (c + 1) * P],
                                                xT_sb[pa][:, kk * P:(kk + 1) * P], start=(kk == 0), stop=(kk == KT - 1))
                last.then_inc(fh_ready, 1)

            def ffn_w2(pa, k):
                e = pe.value_load(r_texp[0:1, bass.ds(k, 1)], min_val=0, max_val=E - 1)
                pe.wait_ge(fg_done, k + 1 + 2)
                pe.wait_ge(fy_done, k + 1)
                for kk in range(FT):
                    last = nc.tensor.matmul(bank(6 + pa)[:, 0:D], hT_sb[pa][:, kk * P:(kk + 1) * P],
                                            w2_sb[:, bass.ds(e * (FT * D) + kk * D, D)], start=(kk == 0), stop=(kk == FT - 1))
                last.then_inc(fy_ready, 1)

            pe.wait_ge(w2_in, 16 * E)
            pe.wait_ge(texp_done, 2)

            def first(k, nth):
                ffn_xt(0, k, nth)
                ffn_w1(0, k)
                ffn_xt(1, k + 1, nth)

            def tiles(k, nth, last):
                for u in range(RING):
                    if u + 1 < RING or not last:
                        ffn_w1((u + 1) % 2, k + u + 1)
                    if u + 2 < RING or not last:
                        ffn_xt((u + 2) % RING, k + u + 2, nth if u + 2 < RING else nth + 16)
                    ffn_w2(u % 2, k + u)

            first(0, 16)
            with pe.Fori(0, NS_MOST // RING - 1) as it:
                tiles(it * RING, it * 16 + 16, False)
            tiles(NS_MOST - RING, 16 * (NS_MOST // RING), True)
            fl = pe.value_load(more[0:1, 0:1], min_val=0, max_val=1)
            with pe.If(fl > 0):
                with pe.Fori(NS_MOST // RING, NS // RING) as it:
                    first(it * RING, it * 16 + 16)
                    tiles(it * RING, it * 16 + 16, True)

        @blk.vector
        def _(v):
            steps = [0]

            def seq(ins):
                steps[0] += 1
                ins.then_inc(dve_step, 1)
                v.wait_ge(dve_step, steps[0])

            v.sem_inc(o_free, 2)
            v.sem_inc(fy_done, 2)
            for pa in range(2):
                v.sem_inc(mx_done[pa], 2)
            nc.vector.memset(xcT[:, :, :, J:JP], 0.0).then_inc(pad_done, 1)

            def statistics(t, src):
                seq(nc.vector.bn_stats(stats[:, t, :], src))
                nc.vector.bn_aggr(mv[:, t, :], stats[:, t, :]).then_inc(dve_step, 1)
                steps[0] += 1

            def variances(c, done):
                v.wait_ge(dve_step, steps[0])
                nc.vector.tensor_scalar_add(ve[:, 4 * c:4 * c + 4], mv[:, 4 * c:4 * c + 4, 1], EPS).then_inc(done, 1)

            def normalise(c, rooted, src, dst, done):
                a, w = rstd[:, 4 * c:4 * c + 4], nt1[:, 4 * c:4 * c + 4]
                v.wait_ge(rooted, c + 1)
                seq(nc.vector.reciprocal(a, a))
                seq(nc.vector.tensor_tensor(w, a, a, ALU.mult))
                seq(nc.vector.tensor_tensor(w, w, ve[:, 4 * c:4 * c + 4], ALU.mult))
                seq(nc.vector.tensor_scalar(w, w, -0.5, 1.5, ALU.mult, ALU.add))
                seq(nc.vector.tensor_tensor(a, a, w, ALU.mult))
                for t in range(4 * c, 4 * c + 4):
                    nc.vector.tensor_scalar(dst(t), src(t), mv[:, t, 0:1], rstd[:, t:t + 1],
                                            ALU.subtract, ALU.mult).then_inc(done, 1)

            def stats_in(c):
                v.wait_ge(x_in[c], 16)
                for t in range(4 * c, 4 * c + 4):
                    nc.vector.bn_stats(stats[:, t, :], xres[:, t, :]).then_inc(dve_step, 1)
                    steps[0] += 1
                v.wait_ge(dve_step, steps[0])
                for t in range(4 * c, 4 * c + 4):
                    nc.vector.bn_aggr(mv[:, t, :], stats[:, t, :]).then_inc(dve_step, 1)
                    steps[0] += 1
                variances(c, ve_done)

            def rows_in(c):
                normalise(c, sqrt_done, lambda t: xres[:, t, :], lambda t: xn[:, t, :], xn_done)

            stats_in(0)
            stats_in(1)
            rows_in(0)
            rows_in(1)
            v.wait_ge(iota_made, 5)

            def indices(op, val):
                if op is None:
                    seq(nc.vector.tensor_copy(fcol[:, :], icol))
                    seq(nc.vector.tensor_copy(frow[:, 0:1], irow[:, :]))
                else:
                    seq(nc.vector.tensor_scalar(ic2, icol, val, None, op))
                    seq(nc.vector.tensor_scalar(ir2[:, :], irow[:, :], val, None, op))
                    seq(nc.vector.tensor_copy(fcol[:, :], ic2))
                    seq(nc.vector.tensor_copy(frow[:, 0:1], ir2[:, :]))

            indices(ALU.logical_shift_right, 4)
            nc.vector.tensor_scalar(heads[:, :], fcol[:, :], frow[:, 0:1], None, ALU.is_equal).then_inc(heads_made, 1)
            v.wait_ge(heads_made, 1)
            stats_in(2)
            stats_in(3)

            def constants():
                v.wait_ge(ident_made, 2)
                nc.vector.tensor_copy(ident_b[:, :], ident[:, :]).then_inc(pad_done, 1)
                indices(ALU.bitwise_and, E - 1)
                seq(nc.vector.tensor_scalar(same_e[:, :], fcol[:, :], frow[:, 0:1], None, ALU.is_equal))
                indices(ALU.logical_shift_right, 3)
                seq(nc.vector.tensor_scalar(prev_e[:, :], fcol[:, :], frow[:, 0:1], None, ALU.is_gt))
                seq(nc.vector.tensor_tensor(prev_e[:, :], prev_e[:, :], same_e[:, :], ALU.mult))
                indices(None, 0)
                seq(nc.vector.tensor_scalar(before[:, :], fcol[:, :], frow[:, 0:1], None, ALU.is_gt))
                seq(nc.vector.tensor_scalar(seen[:, :], fcol[:, :], frow[:, 0:1], None, ALU.is_ge))
                seq(nc.vector.memset(ones_b[:, :], 1.0))
                for i, sh in enumerate(SHIFTS[0] + SHIFTS[1]):
                    seq(nc.vector.tensor_scalar(digit[:, i, :], jint[:, :], float(1 << sh), None, ALU.mult))

            def norm_max(i):
                v.wait_ge(norm_ready, i + 1)
                nc.vector.reduce_max(n2[:, i:i + 1], bank(7)[:, 0:JOBS[QK[i]][4]], AX.X).then_inc(norm_done, 1)

            def bound(b):
                v.wait_ge(norm_done, PER_B * (b + 1))
                for m in range(KT):
                    o = b * PER_B + m * PER_HALF
                    seq(nc.vector.reduce_max(bnd[:, 0:1], n2[:, o:o + 2], AX.X))
                    seq(nc.vector.reduce_max(bnd[:, 1:2], n2[:, o + 2:o + PER_HALF], AX.X))
                    seq(nc.vector.tensor_tensor(bnd[:, 2 + m:3 + m], bnd[:, 0:1], bnd[:, 1:2], ALU.mult))
                nc.vector.tensor_tensor(bmax[:, b:b + 1], bnd[:, 2:3], bnd[:, 3:4], ALU.max).then_inc(bound_done, 1)

            def set_flag(b):
                v.wait_ge(all_max, b + 1)
                limit = (SAFE / SCALE) ** 2 if not force_shift else -1.0
                nc.vector.tensor_scalar(flag[:, b:b + 1], ball[:, b:b + 1], limit, None, ALU.is_gt).then_inc(flag_done, 1)

            for i in range(len(QK)):
                if i == 1:
                    rows_in(2)
                if i == 3:
                    rows_in(3)
                if i == PER_B:
                    norm_max(i - 1)
                    bound(0)
                    constants()
                kind, b, m, n0, w = JOBS[QK[i]]
                v.wait_ge(hi_done, i + 1)
                v.wait_ge(sq_done, i + 1)
                if i >= 2:
                    v.wait_ge(low_done, i - 1)
                nc.vector.tensor_tensor(rem[:, i % 2, 0:w], bank(QK[i] % NBK)[:, 0:w],
                                        piece[:, i % NPIECES, 0, 0:w], ALU.subtract).then_inc(lo_done, 1)
                v.wait_ge(lo_done, i + 1)
                nc.vector.tensor_copy(piece[:, i % NPIECES, 1, 0:w], rem[:, i % 2, 0:w]).then_inc(mid_done, 1)
                if i >= 1 and i != PER_B:
                    norm_max(i - 1)
                if i == 2 * PER_B - 2:
                    set_flag(0)
            norm_max(len(QK) - 1)
            bound(1)
            set_flag(1)

            def take_maxima(pa, g0):
                i = 0
                for r in range(GH):
                    for qt in range(QT):
                        for j, (c0, w) in enumerate(max_pieces(qt)):
                            v.wait_ge(mx_ready[pa], (g0 // 2) * (GH * NPIECE) + i + 1)
                            nc.vector.reduce_max(mx[:, r, qt, j:j + 1], o_ps[pa][:, 512 * (i % 2):512 * (i % 2) + w],
                                                 AX.X).then_inc(mx_done[pa], 1)
                            i += 1
                v.wait_ge(mx_done[pa], (g0 // 2) * (GH * NPIECE) + GH * NPIECE + 2)
                hi = shift[:, :, :, 0].rearrange("p q h -> p h q")
                nc.vector.tensor_reduce(mrow, mx, AX.X, ALU.max, negate=True).then_inc(sh_done[pa], 1)
                v.wait_ge(sh_done[pa], g0 // 2 * 3 + 1)
                nc.vector.tensor_copy(hi, mrow[:, :, :]).then_inc(sh_done[pa], 1)
                v.wait_ge(sh_done[pa], g0 // 2 * 3 + 2)
                nc.vector.tensor_tensor(shift[:, :, :, 1].rearrange("p q h -> p h q"), mrow[:, :, :], hi,
                                        ALU.subtract).then_inc(sh_done[pa], 1)
                v.wait_ge(shT_ready[pa], g0 // 2 + 1)
                nc.vector.tensor_copy(shiftT[:, :], o_ps[pa][0:2 * GH, 0:512].bitcast(BF16)).then_inc(shT_ask[pa], 1)

            def masks(g0):
                for s in range(1, NSTEP):
                    for r in range(GH):
                        v.wait_ge(exp_done, (g0 * NSTEP + s) * GH + r + 1 + 2)
                        for (t, q0, c0) in STEPS[s]:
                            w = min(P, S - q0)
                            off = 0
                            if t == 1:
                                w, off = 2 * P - M, M - P
                            a = pbuf[:, s % 2, r, c0:c0 + w]
                            last = nc.vector.scalar_tensor_tensor(a, a, 3.0e38, seen[:, off:off + w], ALU.min, ALU.mult)
                        last.then_inc(mask_done, 1)

            def take_outputs(pa, g0):
                v.wait_ge(pv_done, g0 * NSTEP + NSTEP + 2)
                nc.vector.tensor_copy(
                    oT[:, bass.ds(g0 // (2 * KT), 1), bass.ds(g0 % (2 * KT), 1), :].rearrange("p b g n -> p (b g n)"),
                    o_ps[pa]).then_inc(o_free, 1)

            def group(pa, g0, before_g=None):
                fl = v.value_load(flag[0:1, bass.ds(g0 // (2 * KT), 1)], min_val=0, max_val=1)
                with v.If(fl > 0):
                    take_maxima(pa, g0)
                if before_g is not None:
                    take_outputs(1 - pa, before_g)
                masks(g0)

            v.wait_ge(biased, TT)
            for i in range(NPIECES):
                v.wait_ge(qk_out[i], 16 * stores(i, 2 * PER_B))
            seq(nc.vector.memset(mx, -3.0e38))
            v.wait_ge(flag_done, 2)
            group(0, 0)
            with v.Fori(0, NG - 1) as it:
                group(1, it * 2 + 1, it * 2)
                group(0, it * 2 + 2, it * 2 + 1)
            group(1, 2 * NG - 1, 2 * NG - 2)
            take_outputs(1, 2 * NG - 1)

            def normalise_heads(t):
                v.wait_ge(ot_ready, t + 1)
                src = bank(t % 2).rearrange("p (g c) -> p g c", c=32)
                if t >= 2:
                    v.wait_ge(ont_ready, t - 1)
                seq(nc.vector.reciprocal(rec[:, t % 2, :], src[:, :, HD]))
                nc.vector.tensor_tensor(on_sb[:, t % 2, :].rearrange("p (h c) -> p h c", c=HD), src[:, :, 0:HD],
                                        rec[:, t % 2, :, None].broadcast_to([P, H, HD]), ALU.mult).then_inc(on_done, 1)

            for t in range(TT + 2):
                if t < TT:
                    normalise_heads(t)
                u = t - 2
                if u >= 0:
                    v.wait_ge(wo_ready, u + 1)
                    nc.vector.tensor_tensor(rows[:, u, D:2 * D], xres[:, u, :], bank(4 + u % 2)[:, 0:D], ALU.add).then_inc(x1_done, 1)
                    v.wait_ge(x1_done, u + 1)
                    statistics(u, rows[:, u, D:2 * D])
                    if u % 4 == 3:
                        variances(u // 4, ve2_done)
                if u % 4 == 0 and u >= 4:
                    normalise(u // 4 - 1, sqrt2_done, lambda i: rows[:, i, D:2 * D], lambda i: rows[:, i, 0:D], xn2_done)
            normalise(TT // 4 - 1, sqrt2_done, lambda i: rows[:, i, D:2 * D], lambda i: rows[:, i, 0:D], xn2_done)
            seq(nc.vector.tensor_copy(tok1[:, :], tok[:, :]))
            seq(nc.vector.tensor_copy(nowhere[:, :], slot_no[:, :]))
            seq(nc.vector.memset(r_one, 1.0))
            rs3 = r_reset.rearrange("p (e t) -> p e t", e=E)
            seq(nc.vector.memset(r_reset, 1.0))
            seq(nc.vector.memset(rs3[:, :, 0:1], 0.0))
            seq(nc.vector.tensor_scalar(r_e8, fcol[:, 0:E], -1.0, float(E), ALU.mult, ALU.add))
            seq(nc.vector.tensor_scalar(r_i128, fcol[:, 0:16], float(P), None, ALU.mult))
            seq(nc.vector.tensor_copy(cand[:, :], digit[:, 0, :]))
            v.wait_ge(lg_ready, TT)
            lg = bank(7)[:, 0:TE].rearrange("p (t e) -> p t e", e=E)
            pr = r_probs.rearrange("p (t e) -> p t e", e=E)
            seq(nc.vector.reduce_max(r_max, lg, AX.X))
            nc.vector.tensor_tensor(pr, lg, r_max[:, :, None].broadcast_to([P, TT, E]), ALU.subtract).then_inc(lsub_done, 1)
            v.wait_ge(lexp_done, 1)
            seq(nc.vector.reduce_sum(r_max, pr, AX.X))
            seq(nc.vector.reciprocal(r_max, r_max))
            nc.vector.tensor_tensor(pr, pr, r_max[:, :, None].broadcast_to([P, TT, E]), ALU.mult).then_inc(probs_done, 1)
            v.wait_ge(pt_ready, 1)
            seq(nc.vector.tensor_copy(r_PT, bank(0)[:, 0:P]))
            bits = r_PT.bitcast(I32)
            seq(nc.vector.tensor_scalar(r_int, bits, LOW, None, ALU.logical_shift_right))
            seq(nc.vector.tensor_copy(r_key[0], r_int))
            i = 0
            for half, shifts in enumerate(SHIFTS):
                if half == 1:
                    seq(nc.vector.scalar_tensor_tensor(r_eq, r_key[0], cand[:, 0:1], r_low, ALU.is_equal, ALU.mult))
                    seq(nc.vector.tensor_scalar(r_sel, r_key[0], cand[:, 0:1], float((1 << LOW) + 1), ALU.is_gt, ALU.mult))
                    seq(nc.vector.tensor_tensor(r_key[1], r_sel, r_eq, ALU.add))
                    seq(nc.vector.tensor_scalar(cand[:, :], digit[:, i, :], 1.0, None, ALU.add))
                for n, sh in enumerate(shifts):
                    for j in range(1, 4):
                        last = nc.vector.tensor_scalar(r_ge[j - 1], r_key[half], cand[:, j:j + 1], 0.0, ALU.is_ge, ALU.add,
                                                       accum_out=cnt_b[:, j - 1:j])
                    last.then_inc(cnt_done, 1)
                    if i == 0:
                        seq(nc.vector.tensor_scalar(r_int, bits, (1 << LOW) - 1, None, ALU.bitwise_and))
                        seq(nc.vector.tensor_scalar(r_low, r_int, 1.0, None, ALU.add))
                    more_bits = n + 1 < len(shifts)
                    if more_bits:
                        nc.vector.tensor_scalar(nxt[:, :], digit[:, i + 1, :], cand[:, 0:1], None, ALU.add).then_inc(dve_step, 1)
                        steps[0] += 1
                    v.wait_ge(tot_ready, i + 1)
                    seq(nc.vector.tensor_scalar(ndig[:, 0:3], bank(1)[:, 0:3], float(CAP) - 0.5, 0.0, ALU.is_ge, ALU.add,
                                                accum_out=ndig[:, 3:4]))
                    c = 4 if more_bits else 1
                    seq(nc.vector.scalar_tensor_tensor(cand[:, 0:c], ndig[:, 3:4].broadcast_to([P, c]), float(1 << sh),
                                                       (nxt if more_bits else cand)[:, 0:c], ALU.mult, ALU.add))
                    i += 1
            thr = cand[:, 0:1]
            seq(nc.vector.tensor_scalar(r_junk, r_key[1], thr, 0.0, ALU.is_gt, ALU.add, accum_out=cnt_b[:, 0:1]))
            nc.vector.tensor_scalar(r_eq, r_key[1], thr, 0.0, ALU.is_equal, ALU.add, accum_out=cnt_b[:, 1:2]).then_inc(cnt_done, 1)
            v.wait_ge(cnt_done, ROUNDS + 1)
            seq(nc.vector.tensor_tensor_scan(r_junk, r_one, r_eq, 0.0, ALU.mult, ALU.add))
            v.wait_ge(tot_ready, ROUNDS + 1)
            seq(nc.vector.tensor_copy(lim[:, 1:2], bank(2)[:, 0:1]))
            seq(nc.vector.tensor_scalar(lim[:, 0:1], bank(1)[:, 0:1], -1.0, float(CAP), ALU.mult, ALU.add))
            seq(nc.vector.tensor_tensor(lim[:, 0:1], lim[:, 0:1], lim[:, 1:2], ALU.subtract))
            seq(nc.vector.scalar_tensor_tensor(r_eq, r_junk, lim[:, 0:1], r_eq, ALU.is_le, ALU.mult))
            nc.vector.scalar_tensor_tensor(r_sel, r_key[1], thr, r_eq, ALU.is_gt, ALU.add).then_inc(sel_done, 1)
            v.wait_ge(selT_ready, 1)
            t3 = r_tmp.rearrange("p (t e) -> p t e", e=E)
            h3 = r_hot.rearrange("p (t e) -> p t e", e=E)
            seq(nc.vector.tensor_copy(r_tmp, bank(0)[:, 0:P]))
            seq(nc.vector.reduce_max(r_any, t3, AX.X))
            seq(nc.vector.tensor_scalar(r_any, r_any, -1.0, 1.0, ALU.mult, ALU.add))
            seq(nc.vector.tensor_tensor(t3, t3, r_any[:, :, None].broadcast_to([P, TT, E]), ALU.add))
            seq(nc.vector.tensor_tensor(h3, t3, pr, ALU.mult))
            seq(nc.vector.scalar_tensor_tensor(r_hot, r_tmp, -1.0, r_hot, ALU.add, ALU.add))
            seq(nc.vector.reduce_max(r_gate, h3, AX.X))
            seq(nc.vector.tensor_tensor(h3, h3, r_gate[:, :, None].broadcast_to([P, TT, E]), ALU.is_equal))
            seq(nc.vector.tensor_tensor(h3, h3, r_e8[:, None, :].broadcast_to([P, TT, E]), ALU.mult))
            seq(nc.vector.reduce_max(r_any, h3, AX.X))
            seq(nc.vector.tensor_tensor(h3, h3, r_any[:, :, None].broadcast_to([P, TT, E]), ALU.is_equal))
            nc.vector.tensor_copy(r_hotb, r_hot).then_inc(hot_done, 1)
            v.wait_ge(hot_done, 1)
            v.wait_ge(rank_ready, 1)
            te3 = r_te.rearrange("p (e t) -> p e t", e=E)
            in3 = r_inc.rearrange("p (e t) -> p e t", e=E)
            seq(nc.vector.tensor_copy(te3, bank(2)[:, 0:TE].rearrange("p (t e) -> p e t", e=E)))
            seq(nc.vector.tensor_tensor_scan(r_inc, r_reset, r_te, 0.0, ALU.mult, ALU.add))
            jk = r_junk.rearrange("p (e t) -> p e t", e=E)
            seq(nc.vector.tensor_tensor(jk, in3[:, :, TT - 1:TT].broadcast_to([P, E, TT]),
                                        r_i128[:, None, :].broadcast_to([P, E, TT]), ALU.is_gt))
            seq(nc.vector.reduce_sum(r_nt, jk, AX.X))
            seq(nc.vector.tensor_tensor_scan(r_end, r_one[:, 0:E], r_nt, 0.0, ALU.mult, ALU.add))
            seq(nc.vector.tensor_tensor(r_nt, r_end, r_nt, ALU.subtract))
            seq(nc.vector.tensor_scalar(r_nt, r_nt, float(P), None, ALU.mult))
            seq(nc.vector.tensor_tensor(in3, in3, te3, ALU.subtract))
            seq(nc.vector.tensor_tensor(in3, in3, r_nt[:, :, None].broadcast_to([P, E, TT]), ALU.add))
            seq(nc.vector.tensor_tensor(t3, bank(1)[:, 0:TE].rearrange("p (t e) -> p t e", e=E),
                                        r_inc.rearrange("p (e t) -> p t e", e=E), ALU.add))
            seq(nc.vector.tensor_tensor(t3, t3, h3, ALU.mult))
            seq(nc.vector.reduce_sum(r_pos, t3, AX.X))
            seq(nc.vector.tensor_copy(r_posi[:, 0, :], r_pos))
            seq(nc.vector.tensor_scalar(r_posi[:, 1, :], r_posi[:, 0, :], P.bit_length() - 1, None, ALU.logical_shift_right))
            seq(nc.vector.tensor_scalar(r_posi[:, 0, :], r_posi[:, 0, :], P - 1, None, ALU.bitwise_and))
            seq(nc.vector.tensor_copy(r_posf[:, :, :], r_posi[:, :, :]))
            seq(nc.vector.tensor_tensor(of_tile, r_posf[:, 1, :, None].broadcast_to([P, TT, NS]),
                                        fcol[:, None, 0:NS].broadcast_to([P, TT, NS]), ALU.is_equal))
            seq(nc.vector.tensor_tensor(hv[:, :, 0, :], of_tile, tok1[:, :, None].broadcast_to([P, TT, NS]), ALU.mult))
            seq(nc.vector.tensor_tensor(hv[:, :, 1, :], of_tile, r_gate[:, :, None].broadcast_to([P, TT, NS]), ALU.mult))
            for t in range(TT):
                if t >= RING:
                    v.wait_ge(slots_ready, t - RING + 1)
                nc.vector.tensor_scalar(in_tile[t % RING], fcol[:, :], r_posf[:, 0, t:t + 1], None, ALU.is_equal).then_inc(tile_made, 1)
            tx = r_tx.rearrange("p (j e) -> p j e", e=E)
            seq(nc.vector.tensor_tensor(tx, r_end[:, None, :].broadcast_to([P, NS, E]),
                                        fcol[:, 0:NS, None].broadcast_to([P, NS, E]), ALU.is_le))
            seq(nc.vector.reduce_sum(r_exp, tx, AX.X))
            nc.vector.tensor_scalar(r_texp[:, :], r_exp, float(E - 1), None, ALU.min).then_inc(texp_done, 1)
            nc.vector.tensor_scalar(more[:, :], r_end[:, E - 1:E], float(NS_MOST), None, ALU.is_gt).then_inc(texp_done, 1)
            v.wait_ge(slots_ready, TT)
            nc.vector.tensor_copy(slot_gate[:, :], bank(3)[:, NS:2 * NS]).then_inc(idx_done, 1)
            seq(nc.vector.scalar_tensor_tensor(nowhere[:, :], bank(3)[:, 0:NS], 0.0, nowhere[:, :], ALU.is_equal, ALU.mult))
            nc.vector.scalar_tensor_tensor(slot_tok[:, :], bank(3)[:, 0:NS], -1.0, nowhere[:, :], ALU.add, ALU.add).then_inc(idx_done, 1)

            def ffn_y(u, k, nth, left):
                v.wait_ge(fy_ready, k + 1 + 2)
                v.wait_ge(xs_in[u], nth)
                if left is not None:
                    v.wait_ge(sent[u], left)
                nc.vector.scalar_tensor_tensor(y_sb[u], bank(6 + u % 2)[:, 0:D], slot_gate[:, bass.ds(k, 1)], xs_sb[u][:, D:XW],
                                               ALU.mult, ALU.add).then_inc(fy_done, 1)

            for u in range(RING):
                ffn_y(u, u, 16, None)
            with v.Fori(1, NS_MOST // RING) as it:
                for u in range(RING):
                    ffn_y(u, it * RING + u, it * 16 + 16, it * 16)
            v.wait_ge(texp_done, 2)
            fl = v.value_load(more[0:1, 0:1], min_val=0, max_val=1)
            with v.If(fl > 0):
                with v.Fori(NS_MOST // RING, NS // RING) as it:
                    for u in range(RING):
                        ffn_y(u, it * RING + u, it * 16 + 16, it * 16)


_INS = ["x", "ctx_1024", "L0_xattn_Wq", "L0_xattn_Wkv", "L0_xattn_Wout", "L0_xattn_bout",
        "L0_ffn_Wg", "L0_ffn_W1", "L0_ffn_W2"]
_OUTS = [((NB, S, D), "float32")]
_SCRATCH = [("token_rows", (T, XW), F32),
            ("q_cut", (NB, KT, 3, P, S), BF16),
            ("k_cut", (NB, KT, 3, P, J), BF16)]


def kernel(**inputs):
    import numpy as _np
    import concourse.bacc as _bacc
    from concourse.bass_utils import run_bass_kernel_spmd as _run

    nc = _bacc.Bacc("TRN2", target_bir_lowering=False, num_devices=1)
    arrays, args = {}, []
    for name in _INS:
        a = _np.ascontiguousarray(inputs[name])
        arrays[f"in_{name}"] = a
        args.append(nc.dram_tensor(f"in_{name}", a.shape, mybir.dt.from_np(a.dtype), kind="ExternalInput").ap())
    for i, (shape, dtype) in enumerate(_OUTS):
        args.append(nc.dram_tensor(f"out_{i}", shape, mybir.dt.from_np(_np.dtype(dtype)), kind="ExternalOutput").ap())
    for name, shape, dtype in _SCRATCH:
        args.append(nc.dram_tensor(name, shape, dtype, kind="Internal").ap())
    xattn_ffn(nc, *args)
    r = _run(nc, [arrays], core_ids=[0])
    return r.results[0]["out_0"]
```
